# Optimizing a Trainium2 kernel written in Bass

```python
import numpy as np
import jax
import jax.numpy as jnp

def _softmax(x, axis=-1):
    return jax.nn.softmax(x, axis=axis)

def _gelu(x):
    return jax.nn.gelu(x, approximate=True)

def _silu(x):
    return jax.nn.silu(x)

def _sigmoid(x):
    return jax.nn.sigmoid(x)

def _layernorm(x, axis=-1, eps=1e-05):
    m = jnp.mean(x, axis=axis, keepdims=True)
    v = jnp.var(x, axis=axis, keepdims=True)
    return (x - m) / jnp.sqrt(v + eps)

def _scatter_add(tgt, idx, src, axis=0):
    return tgt.at[idx].add(src)

def _segment_sum(src, seg, n):
    return jax.ops.segment_sum(src, seg, n)
kernel_name = 'mk_conv_preact_d1_conv_nchw256_r2_ec796a'

def setup_inputs(seed: int=0):
    np.random.seed(seed)
    _w = jnp.asarray

    def _rec_inputs():
        import jax
        import jax.numpy as jnp
        _gk = jax.random.key(seed)
        x = -0.0002928 + 1 * jax.random.normal(jax.random.fold_in(_gk, 1), (4, 128, 32, 32), jnp.float32)
        return x
    x = _rec_inputs()

    def _L0_conv_setup():
        import jax, jax.numpy as jnp
        import numpy as np
        THRESHOLD = 10.0
        K = 24
        EPS = 1e-09
        BN_EPS = 1e-05
        key = jax.random.key(seed)
        k0, k1, k2, k3 = jax.random.split(key, 4)
        B, C, H, W = (4, 128, 32, 32)
        x = jax.random.normal(k0, (B, C, H, W), jnp.float32)
        fc_w = jax.random.normal(k1, (C, C), jnp.float32) * (1.0 / np.sqrt(C))
        fc_b = jax.random.normal(k2, (C,), jnp.float32) * 0.01
        dist_w = jax.random.normal(k3, (32, C), jnp.float32) * (1.0 / np.sqrt(C))
        bn_gamma = jnp.ones((C,), jnp.float32)
        bn_beta = jnp.zeros((C,), jnp.float32)
        return {'x': x, 'fc_w': fc_w, 'fc_b': fc_b, 'dist_w': dist_w, 'bn_gamma': bn_gamma, 'bn_beta': bn_beta}
    _L0_conv_all = _L0_conv_setup()
    _L0_conv_in = {k: v for k, v in _L0_conv_all.items() if k in ('fc_w', 'fc_b', 'dist_w', 'bn_gamma', 'bn_beta')}
    del _L0_conv_all
    return {'x': x, 'L0_conv_fc_w': _L0_conv_in['fc_w'], 'L0_conv_fc_b': _L0_conv_in['fc_b'], 'L0_conv_dist_w': _L0_conv_in['dist_w'], 'L0_conv_bn_gamma': _L0_conv_in['bn_gamma'], 'L0_conv_bn_beta': _L0_conv_in['bn_beta']}

def reference(x, L0_conv_fc_w, L0_conv_fc_b, L0_conv_dist_w, L0_conv_bn_gamma, L0_conv_bn_beta):
    import jax
    import jax.numpy as jnp

    def _L0_conv_ref(x, fc_w, fc_b, dist_w, bn_gamma, bn_beta):
        import jax, jax.numpy as jnp
        import numpy as np
        THRESHOLD = 10.0
        K = 24
        EPS = 1e-09
        BN_EPS = 1e-05
        B, C, H, W = x.shape
        N = H * W
        x_flat = x.reshape(B, C, N).transpose(0, 2, 1)
        emb = jnp.einsum('bnc,ec->bne', x_flat, dist_w)
        sq = jnp.sum(emb * emb, axis=-1)
        d2 = sq[:, :, None] + sq[:, None, :] - 2.0 * jnp.einsum('bne,bme->bnm', emb, emb)
        dist = jnp.sqrt(jnp.clip(d2, 0.0))
        _, idx = jax.lax.top_k(-dist, K)
        bi = jnp.arange(B)[:, None, None]
        ni = jnp.arange(N)[None, :, None]
        knn_mask = jnp.zeros((B, N, N), bool).at[bi, ni, idx].set(True)
        adj = knn_mask & (dist <= THRESHOLD)
        adj = adj | jnp.eye(N, dtype=bool)[None]
        adj_f = adj.astype(x.dtype)
        X_lin = x_flat @ fc_w.T + fc_b
        Dv = jnp.clip(jnp.sum(adj_f, axis=2), EPS, None)
        De = jnp.clip(jnp.sum(adj_f, axis=1), EPS, None)
        H_De_inv = adj_f / De[:, None, :]
        S = H_De_inv @ adj_f.transpose(0, 2, 1) / Dv[:, :, None]
        out_flat = S @ X_lin + x_flat
        out = out_flat.transpose(0, 2, 1).reshape(B, C, H, W)
        mean = jnp.mean(out, axis=(0, 2, 3))
        var = jnp.var(out, axis=(0, 2, 3))
        o = (out - mean[None, :, None, None]) * jax.lax.rsqrt(var[None, :, None, None] + BN_EPS)
        o = o * bn_gamma[None, :, None, None] + bn_beta[None, :, None, None]
        return o * jax.nn.sigmoid(o)

    def _gn(v, G=32, eps=1e-05):
        B_, C_, H_, W_ = v.shape
        g = v.reshape(B_, G, C_ // G, H_, W_)
        m = jnp.mean(g, axis=(2, 3, 4), keepdims=True)
        s = jnp.var(g, axis=(2, 3, 4), keepdims=True)
        return ((g - m) / jnp.sqrt(s + eps)).reshape(v.shape)

    def _ln_c(v, eps=1e-06):
        m = jnp.mean(v, axis=1, keepdims=True)
        s = jnp.var(v, axis=1, keepdims=True)
        return (v - m) / jnp.sqrt(s + eps)

    def _ln_t(v, eps=1e-05):
        m = jnp.mean(v, axis=-1, keepdims=True)
        s = jnp.var(v, axis=-1, keepdims=True)
        return (v - m) / jnp.sqrt(s + eps)

    def _to_tokens(v):
        B_, C_, H_, W_ = v.shape
        return v.reshape(B_, C_, H_ * W_).transpose(0, 2, 1)

    def _from_tokens(t, like):
        B_, C_, H_, W_ = like.shape
        return t.transpose(0, 2, 1).reshape(B_, C_, H_, W_)
    x = x + _L0_conv_ref(_gn(x), L0_conv_fc_w, L0_conv_fc_b, L0_conv_dist_w, L0_conv_bn_gamma, L0_conv_bn_beta)
    return x

_drawn_inputs = setup_inputs


def setup_inputs(seed=0):
    import zlib

    import numpy as np

    out = dict(_drawn_inputs(seed))
    spreads = {'L0_conv_bn_gamma': (1.0, 0.2), 'L0_conv_bn_beta': (0.0, 0.1)}
    factors = {}
    for name, (base, spread) in spreads.items():
        noise = np.random.default_rng([zlib.crc32(name.encode()), seed]).standard_normal(out[name].shape)
        drawn = base * np.exp(spread * noise) if base else spread * noise
        out[name] = jnp.asarray(drawn.astype(out[name].dtype))
    for name, factor in factors.items():
        out[name] = (out[name] * factor).astype(out[name].dtype)
    return out
```

```python
from contextlib import ExitStack

import concourse.bass as bass
from concourse import mybir
from concourse.alu_op_type import AluOpType as ALU
import numpy as np

ACT = mybir.ActivationFunctionType
AX = mybir.AxisListType
F32 = mybir.dt.float32
BF16 = mybir.dt.bfloat16

P = 128
B, C, N, E = 4, 128, 1024, 32
TILES = N // P
HALF = N // 2
TH = TILES // 2
PIECES = 3
NEAREST = 24
GROUP = 4
GN_EPS, BN_EPS, DEG_EPS = 1e-5, 1e-5, 1e-9
KEYS = 4
ROWS = E + 2

LAST_IN = -float(np.nextafter(np.float32(100), np.float32(200))) / 2
FIRST_OUT = -float(np.nextafter(np.float32(-2 * LAST_IN), np.float32(200))) / 2

C_GROUP, C_IDENT, C_SQ, C_BIAS, C_ONE, C_END = 0, P, 2 * P, 2 * P + 64, 2 * P + 65, 2 * P + 66


def constants():
    c = np.zeros((P, C_END), np.float32)
    c[:, C_GROUP:C_GROUP + P] = np.kron(np.eye(P // GROUP), np.full((GROUP, GROUP), 1.0 / GROUP))
    c[:, C_IDENT:C_IDENT + P] = np.eye(P)
    c[0:E, C_SQ + 1] = -0.5
    c[0:E, C_SQ + 32] = -0.5
    c[0, C_BIAS] = 1.0
    c[33, C_BIAS] = 1.0
    c[:, C_ONE] = 1.0
    return c


def build(nc, x, fc_wT, fc_b, dist_wT, gamma, beta, const, out):
    ctx = ExitStack()
    with ctx:
        def sb(name, shape, dt=F32):
            return ctx.enter_context(nc.sbuf_tensor(name, shape, dt))

        def ps(name, shape, dt=F32):
            return ctx.enter_context(nc.psum_tensor(name, shape, dt))

        def sem(name):
            return ctx.enter_context(nc.semaphore(name))

        x_sb = sb("x_sb", [P, B, N])
        xn = sb("xn", [P, B, N])
        xn_cur = sb("xn_cur", [P, N])
        y = sb("y", [P, B, N])
        act_out = sb("act_out", [P, 2, N])
        cst = sb("cst", [P, C_END])
        wT = sb("wT", [P, C])
        bias_row = sb("bias_row", [1, C])
        dT = sb("dT", [P, E])
        gb = sb("gb", [P, 2])
        ident_b = sb("ident_b", [P, P], BF16)
        ones_b = sb("ones_b", [P, 1], BF16)
        ones_row = sb("ones_row", [1, P])
        gn_stats = sb("gn_stats", [P, B, 2, 6])
        gn_mv = sb("gn_mv", [P, B, 2])
        gn_dm = sb("gn_dm", [P, B])
        gn_q = sb("gn_q", [P, B])
        gn_nm = sb("gn_nm", [P, B])
        gn_sd = sb("gn_sd", [P, B])
        gn_rs = sb("gn_rs", [P, B])
        eps_col = sb("eps_col", [P, 1])
        stageL = sb("stageL", [ROWS, N])
        stageR = sb("stageR", [ROWS, N])
        esq = sb("esq", [E, N])
        embL = sb("embL", [ROWS, N])
        embR = sb("embR", [ROWS, N])
        x32 = sb("x32", [P, N])
        xr32 = sb("xr32", [P, N])
        xp = sb("xp", [P, B, TILES, PIECES, C], BF16)
        key = sb("key", [P, KEYS, N])
        keyc = sb("keyc", [P, N])
        work = sb("work", [P, 2, N])
        top = sb("top", [P, 3, 8])
        H = sb("H", [P, 2, N], BF16)
        junk = sb("junk", [P, N], BF16)
        HT = sb("HT", [P, 2, TILES, N], BF16)
        dv = sb("dv", [P, B, TILES])
        rdv = sb("rdv", [P, TILES])
        de = sb("de", [P, TILES])
        rde = sb("rde", [P, TILES])
        t32 = sb("t32", [P, N])
        tr32 = sb("tr32", [P, N])
        tp = sb("tp", [P, PIECES, N], BF16)
        dvb = sb("dvb", [P, N])
        prod = sb("prod", [P, 2, HALF])
        bn_st = sb("bn_st", [P, B * 2, 6])
        bn_mv = sb("bn_mv", [P, 2])
        bn_s = sb("bn_s", [P, 4])

        pg = ps("pg", [P, 2, HALF])
        pt = ps("pt", [P, TILES, C])
        pht = ps("pht", [P, TILES, P], BF16)
        po = ps("po", [P, 2, HALF])
        pd = ps("pd", [P, 512])

        names = ("const_in w_in x_in0 x_in13 out_done setup gstat gmean gdm gvar gsd gscale xn_ready xn_cur_ready "
                 "filled drained emb_staged esq_ready rows_staged stageR_ready emb_live keys_made "
                 "x_hi x_res x_mid x_lo "
                 "key_ready key_used h_ready counted ht_psum ht_copied h_used t_summed t_scaled t_hi t_res "
                 "t_mid t_lo rdv_ready dvb_psum dvb_ready o_ready o_used y_ready step stats_done bn_sd "
                 "bn_affine silu_done sum_done sum_saved").split()
        s = {n: sem("s_" + n) for n in names}

        block = ctx.enter_context(nc.Block())

        AHEAD = 2
        FIRST_PAIRS = 3 + AHEAD
        NEXT_AT = {2: "emb", 3: "sq", 4: "x"}

        def pairs_of_step(b, t, last):
            at = FIRST_PAIRS + (TILES + 3) * b + t + (0 if last else sum(k < t for k in NEXT_AT))
            got = []
            if t + AHEAD < TILES:
                got.append(("key", b, t + AHEAD, at))
                at += 1
            elif not last:
                got.append(("key", b + 1, t + AHEAD - TILES, at))
                at += 1
            if t in NEXT_AT and not last:
                got.append((NEXT_AT[t], b + 1, 0, at))
            return got

        first_pairs = [("emb", 0, 0, 0), ("sq", 0, 0, 1), ("x", 0, 0, 2)] + \
                      [("key", 0, t, 3 + t) for t in range(AHEAD)]

        def images(body):
            for b in range(B):
                body(b, b == 0, b == B - 1)

        @block.sync
        def _(sp):
            sp.dma_start(x_sb[:, 0, :], x[0]).then_inc(s["x_in0"], 16)
            sp.dma_start(x_sb[:, 1:B, :], x[1:B].rearrange("b c n -> c b n")).then_inc(s["x_in13"], 16)
            for b in range(B):
                sp.wait_ge(s["sum_done"], b + 1)
                sp.dma_start(out[b], y[:, b, :]).then_inc(s["out_done"], 16)
            sp.wait_ge(s["out_done"], 16 * B)

        @block.tensor
        def _(pe):
            ident = cst[:, C_IDENT:C_IDENT + P]
            group = cst[:, C_GROUP:C_GROUP + P]
            sqsel = cst[0:E, C_SQ:C_SQ + 64]

            def group_norm(k, a, z):
                pe.wait_ge(s["gstat"], k + 1)
                pe.matmul(po[:, 0, 0:z - a], group, gn_mv[:, a:z, 0], start=True, stop=True).then_inc(s["gmean"], 1)
                pe.wait_ge(s["gdm"], k + 1)
                pe.matmul(po[:, 1, 0:z - a], group, gn_q[:, a:z], start=True, stop=True).then_inc(s["gvar"], 1)

            def fill(kind, b, t, p):
                for h in range(2):
                    cols = slice(h * HALF, (h + 1) * HALF)
                    if kind == "emb" and h == 0:
                        pe.wait_ge(s["xn_cur_ready"], b + 1)
                    if kind == "sq":
                        pe.wait_ge(s["esq_ready"], 2 * b + h + 1)
                    if kind == "key" and t == 0 and h == 0:
                        pe.wait_ge(s["emb_live"], 2 * (b + 1))
                    if not (isinstance(p, int) and p == 0):
                        pe.wait_ge(s["drained"], 2 * (p - 1) + h + 1)
                    if kind == "emb":
                        mm = pe.matmul(pg[0:E, h, :], dT[:, :], xn_cur[:, cols], start=True, stop=True)
                    elif kind == "sq":
                        mm = pe.matmul(pg[0:64, h, :], sqsel, esq[:, cols], start=True, stop=True)
                    elif kind == "key":
                        mm = pe.matmul(pg[:, h, :], embL[:, t * P:(t + 1) * P], embR[:, cols], start=True, stop=True)
                    else:
                        for i in range(TH):
                            o = pg[:, h, i * C:(i + 1) * C]
                            n = h * HALF + i * P
                            pe.matmul(o, xn_cur[:, n:n + P], wT[:, :], start=(i == 0), stop=False, skip_group_check=True)
                            mm = pe.matmul(o, ones_row[:, :], bias_row[:, :], start=False, stop=True, skip_group_check=True)
                    mm.then_inc(s["filled"], 1)
                if kind == "key":
                    pass

            def neighbours(b, t):
                k = b * TILES + t
                pe.wait_ge(s["h_ready"], k + 1)
                if not (isinstance(b, int) and k == 0):
                    pe.wait_ge(s["ht_copied"], k)
                for j in range(TILES):
                    mm = pe.transpose(pht[:, j, :], H[:, t % 2, j * P:(j + 1) * P], ident_b[:, :])
                mm.then_inc(s["ht_psum"], 1)
                if t == 0:
                    pe.wait_ge(s["x_lo"], 2 * (b + 1))
                    if not (isinstance(b, int) and b == 0):
                        pe.wait_ge(s["t_scaled"], b)
                for j in range(TILES):
                    lhs = H[:, t % 2, j * P:(j + 1) * P]
                    for q in range(PIECES):
                        pe.matmul(pt[:, j, :], lhs, xp[:, b, t, q, :], start=(t == 0 and j % TH == 0 and q == 0),
                                  stop=(t == TILES - 1 and q == PIECES - 1), skip_group_check=True)
                    mm = pe.matmul(pd[:, t * TILES + j:t * TILES + j + 1], lhs, ones_b[:, :], start=True, stop=True,
                                   skip_group_check=True)
                mm.then_inc(s["h_used"], 1)

            def spread_dv(b):
                pe.wait_ge(s["rdv_ready"], b + 1)
                for h in range(2):
                    if not (isinstance(b, int) and b == 0):
                        pe.wait_ge(s["o_used"], 2 * (b - 1) + h + 1)
                    for i in range(TH):
                        t = h * TH + i
                        mm = pe.matmul(po[:, h, i * P:(i + 1) * P], rdv[:, t:t + 1].to_broadcast([P, P]), ident,
                                       start=True, stop=True, skip_group_check=True)
                    mm.then_inc(s["dvb_psum"], 1)

            def gather(b, h):
                pe.wait_ge(s["dvb_ready"], 2 * b + h + 1)
                if h == 0:
                    pe.wait_ge(s["t_lo"], 2 * (b + 1))
                    pe.wait_ge(s["ht_copied"], TILES * (b + 1))
                for j in range(TILES):
                    for q in range(PIECES):
                        mm = pe.matmul(po[:, h, :], tp[:, q, j * C:(j + 1) * C], HT[:, b % 2, j, h * HALF:(h + 1) * HALF],
                                       start=(j == 0 and q == 0), stop=(j == TILES - 1 and q == PIECES - 1))
                mm.then_inc(s["o_ready"], 1)

            pe.wait_ge(s["const_in"], 16)
            pe.wait_ge(s["w_in"], 16 * 5)
            pe.wait_ge(s["setup"], 3)
            group_norm(0, 0, 1)
            for f in first_pairs:
                fill(*f)
            group_norm(1, 1, B)

            def image(b, first, last):
                for t in range(TILES):
                    for f in pairs_of_step(b, t, last):
                        fill(*f)
                    neighbours(b, t)
                    if not first:
                        if t == 1:
                            spread_dv(b - 1)
                        if t == 2:
                            gather(b - 1, 0)
                        if t == 4:
                            gather(b - 1, 1)
            images(image)
            spread_dv(B - 1)
            for h in range(2):
                gather(B - 1, h)

        @block.scalar
        def _(act):
            act.dma_start(cst[:, :], const).then_inc(s["const_in"], 16)
            act.dma_start(dT[:, :], dist_wT).then_inc(s["w_in"], 16)
            act.dma_start(wT[:, :], fc_wT).then_inc(s["w_in"], 16)
            act.dma_start(bias_row[:, :], fc_b).then_inc(s["w_in"], 16)
            act.dma_start(gb[:, 0:1], gamma).then_inc(s["w_in"], 16)
            act.dma_start(gb[:, 1:2], beta).then_inc(s["w_in"], 16)
            act.wait_ge(s["setup"], 3)

            def group_sd(k, a, z):
                act.wait_ge(s["gvar"], k + 1)
                act.activation(gn_sd[:, a:z], po[:, 1, 0:z - a], ACT.Sqrt, bias=eps_col[:, :]).then_inc(s["gsd"], 1)

            def drain(kind, b, t, p):
                for h in range(2):
                    cols = slice(h * HALF, (h + 1) * HALF)
                    act.wait_ge(s["filled"], 2 * p + h + 1)
                    if kind == "emb":
                        if h == 0 and not (isinstance(b, int) and b == 0):
                            act.wait_ge(s["emb_live"], 2 * b)
                        act.activation(stageL[0:E, cols], pg[0:E, h, :], ACT.Copy).then_inc(s["emb_staged"], 1)
                        act.activation(esq[:, cols], pg[0:E, h, :], ACT.Square).then_inc(s["esq_ready"], 1)
                        act.wait_ge(s["emb_staged"], 2 * b + h + 1)
                        act.wait_ge(s["esq_ready"], 2 * b + h + 1)
                        act.sem_inc(s["drained"], 1)
                    elif kind == "sq":
                        act.activation(stageL[E:ROWS, cols], pg[0:2, h, :], ACT.Identity,
                                       bias=cst[0:2, C_BIAS:C_BIAS + 1]).then_inc(s["rows_staged"], 1)
                        act.activation(stageR[E:ROWS, cols], pg[32:34, h, :], ACT.Identity,
                                       bias=cst[32:34, C_BIAS:C_BIAS + 1]).then_inc(s["rows_staged"], 1)
                        act.wait_ge(s["rows_staged"], 4 * b + 2 * h + 2)
                        act.sem_inc(s["drained"], 1)
                    elif kind == "x":
                        if not (isinstance(b, int) and b == 0):
                            act.wait_ge(s["x_lo"], 2 * (b - 1) + h + 1)
                        act.activation(x32[:, cols], pg[:, h, :], ACT.Copy).then_inc(s["x_hi"], 1)
                        act.activation(xp[:, b, h * TH:(h + 1) * TH, 0, :],
                                       pg[:, h, :].rearrange("p (t c) -> p t c", c=C), ACT.Copy).then_inc(s["x_hi"], 1)
                        act.wait_ge(s["x_hi"], 4 * b + 2 * h + 2)
                        act.sem_inc(s["drained"], 1)
                    else:
                        k = b * TILES + t
                        if not (isinstance(b, int) and k < KEYS):
                            act.wait_ge(s["key_used"], k - KEYS + 1)
                        act.activation(key[:, t % KEYS, cols], pg[:, h, :], ACT.Copy).then_inc(s["drained"], 1)

            def middle_x(b):
                for h in range(2):
                    act.wait_ge(s["x_res"], 2 * b + h + 1)
                    act.activation(xp[:, b, h * TH:(h + 1) * TH, 1, :],
                                   xr32[:, h * HALF:(h + 1) * HALF].rearrange("p (t c) -> p t c", c=C),
                                   ACT.Copy).then_inc(s["x_mid"], 1)

            def take_tile(b, t):
                k = b * TILES + t
                act.wait_ge(s["h_ready"], k + 1)
                if not (isinstance(b, int) and k == 0):
                    act.wait_ge(s["counted"], k)
                act.activation(junk[:, :], H[:, t % 2, :], ACT.Copy, accum_out=dv[:, b, t:t + 1]).then_inc(s["counted"], 1)
                act.wait_ge(s["ht_psum"], k + 1)
                if t == 0 and not (isinstance(b, int) and b < 2):
                    act.wait_ge(s["o_ready"], 2 * (b - 1))
                act.activation(HT[:, b % 2, :, t * P:(t + 1) * P], pht[:, :, :], ACT.Copy).then_inc(s["ht_copied"], 1)

            def split_t(b):
                for h in range(2):
                    cols = slice(h * HALF, (h + 1) * HALF)
                    act.wait_ge(s["t_scaled"], b + 1)
                    if h == 0 and not (isinstance(b, int) and b == 0):
                        act.wait_ge(s["o_ready"], 2 * b)
                    act.activation(tp[:, 0, cols], t32[:, cols], ACT.Copy).then_inc(s["t_hi"], 1)
                for h in range(2):
                    cols = slice(h * HALF, (h + 1) * HALF)
                    act.wait_ge(s["t_res"], 2 * b + h + 1)
                    act.activation(tp[:, 1, cols], tr32[:, cols], ACT.Copy).then_inc(s["t_mid"], 1)

            def copy_dv(b):
                for h in range(2):
                    act.wait_ge(s["dvb_psum"], 2 * b + h + 1)
                    act.activation(dvb[:, h * HALF:(h + 1) * HALF], po[:, h, :], ACT.Copy).then_inc(s["dvb_ready"], 1)

            group_sd(0, 0, 1)
            for f in first_pairs:
                drain(*f)
            middle_x(0)
            group_sd(1, 1, B)

            def image(b, first, last):
                for t in range(TILES):
                    for f in pairs_of_step(b, t, last):
                        drain(*f)
                    if t == 5 and not last:
                        middle_x(b + 1)
                    take_tile(b, t)
                    if not first and t == 1:
                        copy_dv(b - 1)
                split_t(b)
            images(image)
            copy_dv(B - 1)
            act.wait_ge(s["stats_done"], 2)
            act.activation(bn_s[:, 0:1], bn_mv[:, 1:2], ACT.Sqrt, bias=eps_col[:, :]).then_inc(s["bn_sd"], 1)
            act.wait_ge(s["bn_affine"], 1)
            for b in range(B):
                if b >= 2:
                    act.wait_ge(s["sum_done"], b - 1)
                act.activation(act_out[:, b % 2, :], y[:, b, :], ACT.Silu, scale=bn_s[:, 2:3],
                               bias=bn_s[:, 3:4]).then_inc(s["silu_done"], 1)

        @block.gpsimd
        def _(pool):
            pool.memset(ones_row[:, :], 1.0).then_inc(s["setup"], 1)
            pool.memset(ones_b[:, :], 1.0).then_inc(s["setup"], 1)
            pool.memset(eps_col[:, :], GN_EPS).then_inc(s["setup"], 1)
            pool.wait_ge(s["const_in"], 16)
            pool.tensor_copy(ident_b[:, :], cst[:, C_IDENT:C_IDENT + P]).then_inc(s["setup"], 1)

            def normalise(b):
                pool.tensor_scalar(xn[:, b, :], x_sb[:, b, :], gn_nm[:, b:b + 1], gn_rs[:, b:b + 1],
                                   ALU.add, ALU.mult).then_inc(s["xn_ready"], 1)

            def current(b):
                pool.wait_ge(s["xn_ready"], b + 1)
                if not (isinstance(b, int) and b == 0):
                    pool.wait_ge(s["filled"], 2 * (FIRST_PAIRS + (TILES + 3) * (b - 2) + 7 + 1) if not isinstance(b, int) or b > 1 else 6)
                pool.tensor_copy(xn_cur[:, :], xn[:, b, :]).then_inc(s["xn_cur_ready"], 1)

            def stage(b):
                pool.wait_ge(s["emb_staged"], 2 * (b + 1))
                pool.tensor_copy(stageR[0:E, :], stageL[0:E, :]).then_inc(s["stageR_ready"], 1)

            def make_live(b):
                pool.wait_ge(s["stageR_ready"], b + 1)
                pool.wait_ge(s["rows_staged"], 4 * (b + 1))
                if not (isinstance(b, int) and b == 0):
                    pool.wait_ge(s["filled"], 2 * (FIRST_PAIRS + (TILES + 3) * (b - 1) + 8 + 1))
                pool.tensor_copy(embL[:, :], stageL[:, :]).then_inc(s["emb_live"], 1)
                pool.tensor_copy(embR[:, :], stageR[:, :]).then_inc(s["emb_live"], 1)

            def split(hi, res, mid, lo, b, full, rest, piece):
                for h in range(2):
                    pool.wait_ge(s[hi], (2 * (2 * b + h) + 2) if hi == "x_hi" else 2 * b + h + 1)
                    pool.tensor_tensor(rest(h), full(h), piece(h, 0), ALU.subtract).then_inc(s[res], 1)
                for h in range(2):
                    pool.wait_ge(s[mid], 2 * b + h + 1)
                    pool.tensor_tensor(piece(h, 2), rest(h), piece(h, 1), ALU.subtract).then_inc(s[lo], 1)

            def split_x(b):
                tiles = lambda a, h: a[:, h * HALF:(h + 1) * HALF].rearrange("p (t c) -> p t c", c=C)
                split("x_hi", "x_res", "x_mid", "x_lo", b, lambda h: tiles(x32, h), lambda h: tiles(xr32, h),
                      lambda h, q: xp[:, b, h * TH:(h + 1) * TH, q, :])

            def split_t(b):
                cols = lambda h: slice(h * HALF, (h + 1) * HALF)
                split("t_hi", "t_res", "t_mid", "t_lo", b, lambda h: t32[:, cols(h)], lambda h: tr32[:, cols(h)],
                      lambda h, q: tp[:, q, cols(h)])

            def residual(b, h):
                pool.wait_ge(s["o_used"], 2 * b + h + 1)
                pool.tensor_tensor(y[:, b, h * HALF:(h + 1) * HALF], prod[:, h, :], xn[:, b, h * HALF:(h + 1) * HALF],
                                   ALU.add).then_inc(s["y_ready"], 1)

            pool.wait_ge(s["gscale"], 1)
            pool.wait_ge(s["x_in0"], 16)
            normalise(0)
            current(0)
            stage(0)
            make_live(0)
            split_x(0)
            pool.wait_ge(s["gscale"], 2)
            pool.wait_ge(s["x_in13"], 16)
            for b in range(1, B):
                normalise(b)

            def image(b, first, last):
                if not last:
                    current(b + 1)
                if not first:
                    for h in range(2):
                        residual(b - 1, h)
                if not last:
                    stage(b + 1)
                    split_x(b + 1)
                    make_live(b + 1)
                split_t(b)
            images(image)
            for h in range(2):
                residual(B - 1, h)

        @block.vector
        def _(dve):
            chain = [0]

            def link(ins):
                chain[0] += 1
                ins.then_inc(s["step"], 1)
                dve.wait_ge(s["step"], chain[0])

            def group_stats(k, a, z):
                for b in range(a, z):
                    for h in range(2):
                        ins = dve.bn_stats(gn_stats[:, b, h, :], x_sb[:, b, h * HALF:(h + 1) * HALF])
                link(ins)
                for b in range(a, z):
                    ins = dve.bn_aggr(gn_mv[:, b, :], gn_stats[:, b, :, :])
                chain[0] += 1
                ins.then_inc(s["step"], 1)
                dve.wait_ge(s["step"], chain[0])
                dve.sem_inc(s["gstat"], 1)

            def group_scale(k, a, z):
                dve.wait_ge(s["gmean"], k + 1)
                dve.tensor_tensor(gn_dm[:, a:z], gn_mv[:, a:z, 0], po[:, 0, 0:z - a], ALU.subtract)
                link(dve.tensor_scalar(gn_nm[:, a:z], po[:, 0, 0:z - a], -1.0, None, ALU.mult))
                link(dve.tensor_tensor(gn_q[:, a:z], gn_dm[:, a:z], gn_dm[:, a:z], ALU.mult))
                dve.tensor_tensor(gn_q[:, a:z], gn_q[:, a:z], gn_mv[:, a:z, 1], ALU.add).then_inc(s["gdm"], 1)
                dve.wait_ge(s["gsd"], k + 1)
                dve.reciprocal(gn_rs[:, a:z], gn_sd[:, a:z]).then_inc(s["gscale"], 1)

            def nearest(b, t, last):
                k = b * TILES + t
                dve.wait_ge(s["drained"], 2 * key_pair(b, t, last) + 2)
                link(dve.tensor_scalar(keyc[:, :], key[:, t % KEYS, :], 0.0, FIRST_OUT, ALU.min, ALU.max))
                src = keyc[:, :]
                for r in range(3):
                    link(dve.max(top[:, r, :], src))
                    dst = work[:, r % 2, :]
                    link(dve.match_replace(dst, top[:, r, :], src, FIRST_OUT))
                    src = dst
                if not (isinstance(b, int) and k < 2):
                    dve.wait_ge(s["h_used"], k - 1)
                    dve.wait_ge(s["counted"], k - 1)
                ins = dve.tensor_tensor(H[:, t % 2, :], keyc[:, :], src, ALU.is_gt)
                chain[0] += 1
                ins.then_inc(s["step"], 1)
                dve.wait_ge(s["step"], chain[0])
                dve.sem_inc(s["key_used"], 1)
                blk = H[:, t % 2, t * P:(t + 1) * P]
                dve.tensor_tensor(blk, blk, ident_b[:, :], ALU.max).then_inc(s["h_ready"], 1)

            def key_pair(b, t, last):
                if isinstance(b, int) and b == 0 and t < AHEAD:
                    return 3 + t
                if t < AHEAD:
                    return pairs_of_step(b - 1, t + TILES - AHEAD, False)[0][3]
                return pairs_of_step(b, t - AHEAD, last)[0][3]

            def scale_t(b):
                dve.wait_ge(s["h_used"], TILES * (b + 1))
                if not (isinstance(b, int) and b == 0):
                    dve.wait_ge(s["t_lo"], 2 * b)
                link(dve.tensor_reduce(de[:, :], pd[:, 0:TILES * TILES].rearrange("p (t j) -> p j t", j=TILES),
                                       AX.X, ALU.add))
                link(dve.tensor_scalar(de[:, :], de[:, :], DEG_EPS, None, ALU.max))
                link(dve.reciprocal(rde[:, :], de[:, :]))
                dve.tensor_tensor(t32[:, :].rearrange("p (j c) -> p j c", c=C), pt[:, :, :],
                                  rde[:, :].unsqueeze(2).to_broadcast([P, TILES, C]), ALU.mult).then_inc(s["t_scaled"], 1)
                dve.wait_ge(s["counted"], TILES * (b + 1))
                if not (isinstance(b, int) and b == 0):
                    dve.wait_ge(s["dvb_psum"], 2 * b)
                link(dve.tensor_scalar(rdv[:, :], dv[:, b, :], DEG_EPS, None, ALU.max))
                dve.reciprocal(rdv[:, :], rdv[:, :]).then_inc(s["rdv_ready"], 1)

            def out_half(b, h):
                dve.wait_ge(s["o_ready"], 2 * b + h + 1)
                if not (isinstance(b, int) and b == 0):
                    dve.wait_ge(s["y_ready"], 2 * (b - 1) + h + 1)
                dve.tensor_tensor(prod[:, h, :], po[:, h, :], dvb[:, h * HALF:(h + 1) * HALF],
                                  ALU.mult).then_inc(s["o_used"], 1)

            def y_stats(b, h):
                dve.wait_ge(s["y_ready"], 2 * b + h + 1)
                link(dve.bn_stats(bn_st[:, 2 * b + h, :], y[:, b, h * HALF:(h + 1) * HALF]))

            dve.wait_ge(s["x_in0"], 16)
            group_stats(0, 0, 1)
            group_scale(0, 0, 1)
            dve.wait_ge(s["x_in13"], 16)
            group_stats(1, 1, B)
            group_scale(1, 1, B)
            dve.wait_ge(s["setup"], 4)

            def image(b, first, last):
                for t in range(TILES):
                    nearest(b, t, last)
                    if not first:
                        if t == 3:
                            out_half(b - 1, 0)
                        if t == 5:
                            out_half(b - 1, 1)
                            y_stats(b - 1, 0)
                        if t == 6:
                            y_stats(b - 1, 1)
                scale_t(b)
            images(image)
            for h in range(2):
                out_half(B - 1, h)
            for h in range(2):
                y_stats(B - 1, h)
            dve.bn_aggr(bn_mv[:, :], bn_st[:, :, :]).then_inc(s["stats_done"], 2)
            dve.wait_ge(s["bn_sd"], 1)
            dve.wait_ge(s["w_in"], 16 * 5)
            link(dve.reciprocal(bn_s[:, 1:2], bn_s[:, 0:1]))
            link(dve.tensor_tensor(bn_s[:, 2:3], bn_s[:, 1:2], gb[:, 0:1], ALU.mult))
            link(dve.tensor_tensor(bn_s[:, 0:1], bn_s[:, 2:3], bn_mv[:, 0:1], ALU.mult))
            dve.tensor_tensor(bn_s[:, 3:4], gb[:, 1:2], bn_s[:, 0:1], ALU.subtract).then_inc(s["bn_affine"], 1)
            for b in range(B):
                dve.wait_ge(s["silu_done"], b + 1)
                dve.tensor_tensor(y[:, b, :], act_out[:, b % 2, :], x_sb[:, b, :], ALU.add).then_inc(s["sum_done"], 1)


def kernel(x, L0_conv_fc_w, L0_conv_fc_b, L0_conv_dist_w, L0_conv_bn_gamma, L0_conv_bn_beta):
    import concourse.bacc as bacc
    from concourse.bass_utils import run_bass_kernel_spmd

    arrays = {
        "x": np.ascontiguousarray(x).reshape(B, C, N),
        "fc_wT": np.ascontiguousarray(np.transpose(L0_conv_fc_w)),
        "fc_b": np.ascontiguousarray(L0_conv_fc_b).reshape(1, C),
        "dist_wT": np.ascontiguousarray(np.transpose(L0_conv_dist_w)),
        "gamma": np.ascontiguousarray(L0_conv_bn_gamma).reshape(C, 1),
        "beta": np.ascontiguousarray(L0_conv_bn_beta).reshape(C, 1),
        "const": constants(),
    }
    nc = bacc.Bacc("TRN2", target_bir_lowering=False, num_devices=1)
    args = [nc.dram_tensor(k, a.shape, mybir.dt.from_np(a.dtype), kind="ExternalInput").ap()
            for k, a in arrays.items()]
    out = nc.dram_tensor("out", (B, C, N), F32, kind="ExternalOutput").ap()
    build(nc, *args, out)
    r = run_bass_kernel_spmd(nc, [arrays], core_ids=[0])
    return r.results[0]["out"].reshape(B, C, 32, 32)
```

```python
from contextlib import ExitStack

import concourse.bass as bass
from concourse import mybir
from concourse.alu_op_type import AluOpType as ALU
import numpy as np

ACT = mybir.ActivationFunctionType
AX = mybir.AxisListType
F32 = mybir.dt.float32
BF16 = mybir.dt.bfloat16

P = 128
B, C, N, E = 4, 128, 1024, 32
TILES = N // P
HALF = N // 2
TH = TILES // 2
PIECES = 3
NEAREST = 24
CHUNK = 64
CHUNKS = N // CHUNK
GROUP = 4
GN_EPS, BN_EPS, DEG_EPS = 1e-5, 1e-5, 1e-9
KEYS = 8
HS = 4
LAG = 2
AHEAD = LAG + 2
Q = P // E
QN = N // Q

LAST_IN = -float(np.nextafter(np.float32(100), np.float32(200))) / 2
FIRST_OUT = -float(np.nextafter(np.float32(-2 * LAST_IN), np.float32(200))) / 2
OVER_BITS = int(np.float32(NEAREST + 0.5).view(np.int32))

C_GROUP, C_IDENT, C_SQ, C_END = 0, P, 2 * P, 3 * P
LA, RA, LB, RB = range(4)
SQ_ROW = 2 * E
K_B = SQ_ROW + 2 * PIECES


def constants():
    c = np.zeros((P, C_END), np.float32)
    c[:, C_GROUP:C_GROUP + P] = np.kron(np.eye(P // GROUP), np.full((GROUP, GROUP), 1.0 / GROUP))
    c[:, C_IDENT:C_IDENT + P] = np.eye(P)
    c[:, C_SQ:C_SQ + P] = np.kron(np.eye(Q), np.full((E, E), -0.5))
    return c


def halves(b=None):
    return [(h, slice(h * HALF, (h + 1) * HALF)) for h in range(2)]


def build(nc, x, fc_wT, fc_b, dist_wT, gamma, beta, const, scratch, out):
    ctx = ExitStack()
    with ctx:
        def sb(name, shape, dt=F32):
            return ctx.enter_context(nc.sbuf_tensor(name, shape, dt))

        def ps(name, shape, dt=F32):
            return ctx.enter_context(nc.psum_tensor(name, shape, dt))

        def sem(name):
            return ctx.enter_context(nc.semaphore(name))

        x_sb = sb("x_sb", [P, B, N])
        xn = sb("xn", [P, B, N])
        y = sb("y", [P, B, N])
        cst = sb("cst", [P, C_END])
        wT = sb("wT", [P, C])
        dT = sb("dT", [P, E])
        gb = sb("gb", [P, 2])
        bias_row = sb("bias_row", [1, C])
        bias_r = sb("bias_r", [1, C])
        bias_p1 = sb("bias_p1", [1, PIECES, C], BF16)
        bias_p = sb("bias_p", [PIECES, C], BF16)
        ident_b = sb("ident_b", [P, P], BF16)
        ones_b = sb("ones_b", [P, P], BF16)
        gn_stats = sb("gn_stats", [P, B, 2, 6])
        gn_mv = sb("gn_mv", [P, B, 2])
        gn_dm = sb("gn_dm", [P, B])
        gn_q = sb("gn_q", [P, B])
        gn_nm = sb("gn_nm", [P, B])
        gn_sd = sb("gn_sd", [P, B])
        gn_rs = sb("gn_rs", [P, B])
        eps_col = sb("eps_col", [P, 1])
        esq = sb("esq", [P, QN])
        e32 = sb("e32", [P, 2, QN])
        er32 = sb("er32", [P, 2, QN])
        ep = sb("ep", [P, PIECES, 2, QN], BF16)
        lr = sb("lr", [P, 2, 4, N], BF16)
        x32 = sb("x32", [P, N])
        xr32 = sb("xr32", [P, N])
        xp = sb("xp", [P, 2, TILES, PIECES, C], BF16)
        key = sb("key", [P, KEYS, N])
        cand = sb("cand", [P, CHUNKS, 8])
        cwork = sb("cwork", [P, 2, CHUNKS * 8])
        top = sb("top", [P, 3, 8])
        thr = sb("thr", [P, 1])
        keyc = sb("keyc", [P, N])
        work = sb("work", [P, N])
        H = sb("H", [P, HS, N], BF16)
        junk = sb("junk", [P, N], BF16)
        most = sb("most", [P, TILES])
        HT = sb("HT", [P, 2, TILES, N], BF16)
        dv = sb("dv", [P, B, TILES])
        rdv = sb("rdv", [P, TILES])
        de = sb("de", [P, TILES])
        rde = sb("rde", [P, TILES])
        t32 = sb("t32", [P, N])
        tr32 = sb("tr32", [P, N])
        tp = sb("tp", [P, PIECES, N], BF16)
        dvb = sb("dvb", [P, N])
        prod = sb("prod", [P, 2, HALF])
        bn_st = sb("bn_st", [P, B * 2, 6])
        bn_mv = sb("bn_mv", [P, 2])
        bn_s = sb("bn_s", [P, 4])

        pg = ps("pg", [P, 2, HALF])
        pt = ps("pt", [P, TILES, C])
        pht = ps("pht", [P, TILES, P], BF16)
        po = ps("po", [P, 2, HALF])
        pd = ps("pd", [P, 512])

        names = ("const_in w_in x_in0 x_in13 out_done setup ones_rows bias_split bias_in gstat gmean gdm gvar gsd gscale "
                 "xn_ready filled drained e_sq e_copied e_hi e_res e_mid e_lo ep_out lr_in "
                 "x_hi x_res x_mid x_lo masked eyed counted flagged checked key_used "
                 "h_ready ht_psum ht_copied h_used t_scaled t_hi t_res "
                 "t_mid t_lo rdv_ready dvb_psum dvb_ready o_ready o_used y_ready step slow_step stats_done bn_sd "
                 "bn_affine silu_done sum_done").split()
        s = {n: sem("s_" + n) for n in names}

        block = ctx.enter_context(nc.Block())

        FIRST_PAIRS = 2 + AHEAD
        NEXT = 2
        LR_DMAS = 16 * 14
        first_pairs = [("emb", 0, 0, 0), ("nsq", 0, 0, 0), ("x", 0, 0, 1)] + \
                      [("key", 0, t, 2 + t) for t in range(AHEAD)]

        def pairs_of_step(b, t, last):
            at = FIRST_PAIRS + (TILES + NEXT) * b + t + (0 if last else (t > 0) + (t > 3))
            got = []
            if t == 1 and not last:
                got.append(("nsq", b + 1, 0, at - 1))
            if t + AHEAD < TILES:
                got.append(("key", b, t + AHEAD, at))
            elif not last:
                got.append(("key", b + 1, t + AHEAD - TILES, at))
            if t == 0 and not last:
                got.append(("emb", b + 1, 0, at + 1))
            if t == 3 and not last:
                got.append(("x", b + 1, 0, at + 1))
            return got

        def key_pair(b, t, last):
            if isinstance(b, int) and b == 0 and t < AHEAD:
                return 2 + t
            of, at = (b - 1, t + TILES - AHEAD) if t < AHEAD else (b, t - AHEAD)
            return [p for k, _, _, p in pairs_of_step(of, at, last and t >= AHEAD) if k == "key"][0]

        def after(b, first):
            return not (isinstance(b, int) and b <= first)

        def images(body):
            for b in range(B):
                body(b, b == 0, b == B - 1)

        @block.sync
        def _(sp):
            sp.dma_start(x_sb[:, 0, :], x[0]).then_inc(s["x_in0"], 16)
            sp.dma_start(x_sb[:, 1:B, :], x[1:B].rearrange("b c n -> c b n")).then_inc(s["x_in13"], 16)

            def place(b):
                q = b % 2
                if after(b, 1):
                    sp.wait_ge(s["filled"], 2 * key_pair(b - 2, TILES - 1, False) + 2)

                sp.wait_ge(s["e_lo"], b + 1)
                if after(b, 0):
                    sp.wait_ge(s["lr_in"], LR_DMAS * b)
                sp.dma_start(scratch, ep[:, :, :, :]).then_inc(s["ep_out"], 16)
                sp.wait_ge(s["ep_out"], 16 * (b + 1))
                emb = scratch[:, :, 0, :].rearrange("(q e) p c -> p e q c", e=E)
                nsq = scratch[0:P:E, :, 1, :].rearrange("q p c -> p q c")
                for k, row, piece in ((LA, 0, 0), (LA, 1, 0), (LA, 2, 0), (LA, 3, 1), (RA, 3, 0), (LB, 0, 1), (LB, 1, 2),
                                      (RB, 0, 1), (RB, 1, 0)):
                    sp.dma_start(lr[row * E:(row + 1) * E, q, k, :], emb[piece]).then_inc(s["lr_in"], 16)
                for piece in range(PIECES):
                    sp.dma_start(lr[piece * E:(piece + 1) * E, q, RA, :], emb[piece]).then_inc(s["lr_in"], 16)
                sp.dma_start(lr[SQ_ROW:SQ_ROW + PIECES, q, LB, :], nsq).then_inc(s["lr_in"], 16)
                sp.dma_start(lr[SQ_ROW + PIECES:K_B, q, RB, :], nsq).then_inc(s["lr_in"], 16)

            sp.wait_ge(s["bias_split"], PIECES)
            for q in range(PIECES):
                sp.dma_start(bias_p[q:q + 1, :], bias_p1[0:1, q, :]).then_inc(s["bias_in"], 16)
            sp.wait_ge(s["ones_rows"], 2)
            place(0)

            def image(b, first, last):
                if not last:
                    place(b + 1)
            images(image)
            for b in range(B):
                sp.wait_ge(s["sum_done"], b + 1)
                sp.dma_start(out[b], y[:, b, :]).then_inc(s["out_done"], 16)
            sp.wait_ge(s["out_done"], 16 * B)

        
        @block.tensor
        def _(pe):
            ident = cst[:, C_IDENT:C_IDENT + P]
            group = cst[:, C_GROUP:C_GROUP + P]
            sqsum = cst[:, C_SQ:C_SQ + P]

            def group_norm(k, a, z):
                pe.wait_ge(s["gstat"], k + 1)
                pe.matmul(po[:, 0, 0:z - a], group, gn_mv[:, a:z, 0], start=True, stop=True).then_inc(s["gmean"], 1)
                pe.wait_ge(s["gdm"], k + 1)
                pe.matmul(po[:, 1, 0:z - a], group, gn_q[:, a:z], start=True, stop=True).then_inc(s["gvar"], 1)

            def fill(kind, b, t, p):
                def bank_free(h):
                    if not (isinstance(p, int) and p == 0):
                        pe.wait_ge(s["drained"], 2 * (p - 1) + h + 1)
                if kind == "emb":
                    pe.wait_ge(s["xn_ready"], b + 1)
                    bank_free(0)
                    for q in range(Q):
                        mm = pe.matmul(pg[q * E:(q + 1) * E, 0, 0:QN], dT[:, :], xn[:, b, q * QN:(q + 1) * QN],
                                       start=True, stop=True)
                    mm.then_inc(s["filled"], 1)
                if kind == "nsq":
                    pe.wait_ge(s["e_sq"], b + 1)
                    bank_free(1)
                    pe.matmul(pg[:, 1, 0:QN], sqsum, esq[:, :], start=True, stop=True).then_inc(s["filled"], 1)
                if kind == "x":
                    for h, cols in halves():
                        bank_free(h)
                        for i in range(TH):
                            o = pg[:, h, i * C:(i + 1) * C]
                            n = h * HALF + i * P
                            pe.matmul(o, xn[:, b, n:n + P], wT[:, :], start=(i == 0), stop=False,
                                      skip_group_check=True)
                            mm = pe.matmul(o, ones_b[0:PIECES, :], bias_p[:, :], start=False, stop=True,
                                           skip_group_check=True)
                        mm.then_inc(s["filled"], 1)
                if kind == "key":
                    if t == 0:
                        pe.wait_ge(s["lr_in"], LR_DMAS * (b + 1))
                    for h, cols in halves():
                        bank_free(h)
                        for k, rows, start in ((LA, P, True), (LB, K_B, False)):
                            mm = pe.matmul(pg[:, h, :], lr[0:rows, b % 2, k, t * P:(t + 1) * P],
                                           lr[0:rows, b % 2, k + 1, cols], start=start, stop=not start)
                        mm.then_inc(s["filled"], 1)

            def transpose(b, t):
                k = b * TILES + t
                pe.wait_ge(s["h_ready"], k + 1)
                if after(k, 0):
                    pe.wait_ge(s["ht_copied"], k)
                for j in range(TILES):
                    mm = pe.transpose(pht[:, j, :], H[:, t % HS, j * P:(j + 1) * P], ident_b[:, :])
                mm.then_inc(s["ht_psum"], 1)

            def scatter(b, t):
                if t == 0:
                    pe.wait_ge(s["x_lo"], 2 * (b + 1))
                    if after(b, 0):
                        pe.wait_ge(s["t_scaled"], 2 * b)
                for j in range(TILES):
                    lhs = H[:, t % HS, j * P:(j + 1) * P]
                    for q in range(PIECES):
                        pe.matmul(pt[:, j, :], lhs, xp[:, b % 2, t, q, :], start=(t == 0 and j % TH == 0 and q == 0),
                                  stop=(t == TILES - 1 and q == PIECES - 1), skip_group_check=True)
                    mm = pe.matmul(pd[:, t * TILES + j:t * TILES + j + 1], lhs, ones_b[:, 0:1], start=True, stop=True,
                                   skip_group_check=True)
                mm.then_inc(s["h_used"], 1)

            def spread_dv(b):
                pe.wait_ge(s["rdv_ready"], b + 1)
                for h in range(2):
                    if after(b, 0):
                        pe.wait_ge(s["o_used"], 2 * (b - 1) + h + 1)
                    for i in range(TH):
                        t = h * TH + i
                        mm = pe.matmul(po[:, h, i * P:(i + 1) * P], rdv[:, t:t + 1].to_broadcast([P, P]), ident,
                                       start=True, stop=True, skip_group_check=True)
                    mm.then_inc(s["dvb_psum"], 1)

            def gather(b, h):
                pe.wait_ge(s["dvb_ready"], 2 * b + h + 1)
                if h == 0:
                    pe.wait_ge(s["t_lo"], 2 * (b + 1))
                    pe.wait_ge(s["ht_copied"], TILES * (b + 1))
                for j in range(TILES):
                    for q in range(PIECES):
                        mm = pe.matmul(po[:, h, :], tp[:, q, j * C:(j + 1) * C],
                                       HT[:, b % 2, j, h * HALF:(h + 1) * HALF],
                                       start=(j == 0 and q == 0), stop=(j == TILES - 1 and q == PIECES - 1))
                mm.then_inc(s["o_ready"], 1)

            pe.wait_ge(s["const_in"], 16)
            pe.wait_ge(s["w_in"], 16 * 5)
            pe.wait_ge(s["setup"], 4)
            group_norm(0, 0, 1)
            pe.wait_ge(s["bias_in"], 16 * PIECES)
            for f in first_pairs:
                fill(*f)
            group_norm(1, 1, B)

            def image(b, first, last):
                for t in range(TILES):
                    for f in pairs_of_step(b, t, last):
                        fill(*f)
                    transpose(b, t)
                    if not first and t == 0:
                        spread_dv(b - 1)
                    scatter(b, t)
                    if not first and t == 2:
                        gather(b - 1, 0)
                    if not first and t == 4:
                        gather(b - 1, 1)
            images(image)
            spread_dv(B - 1)
            for h in range(2):
                gather(B - 1, h)

        @block.scalar
        def _(act):
            act.dma_start(cst[:, :], const).then_inc(s["const_in"], 16)
            act.dma_start(dT[:, :], dist_wT).then_inc(s["w_in"], 16)
            act.dma_start(wT[:, :], fc_wT).then_inc(s["w_in"], 16)
            act.dma_start(bias_row[:, :], fc_b).then_inc(s["w_in"], 16)
            act.dma_start(gb[:, 0:1], gamma).then_inc(s["w_in"], 16)
            act.dma_start(gb[:, 1:2], beta).then_inc(s["w_in"], 16)
            act.wait_ge(s["setup"], 4)

            def group_sd(k, a, z):
                act.wait_ge(s["gvar"], k + 1)
                act.activation(gn_sd[:, a:z], po[:, 1, 0:z - a], ACT.Sqrt, bias=eps_col[:, :]).then_inc(s["gsd"], 1)

            def drain(kind, b, t, p):
                if kind == "emb":
                    act.wait_ge(s["filled"], 2 * p + 1)
                    act.activation(esq[:, :], pg[:, 0, 0:QN], ACT.Square).then_inc(s["e_sq"], 1)
                if kind == "nsq":
                    act.wait_ge(s["filled"], 2 * p + 2)
                    if after(b, 0):
                        act.wait_ge(s["e_lo"], b)
                        act.wait_ge(s["lr_in"], LR_DMAS * b)
                    act.activation(e32[:, :, :], pg[:, :, 0:QN], ACT.Copy).then_inc(s["e_copied"], 1)
                    act.wait_ge(s["e_copied"], b + 1)
                    act.activation(ep[:, 0, :, :], e32[:, :, :], ACT.Copy).then_inc(s["e_hi"], 1)
                    act.sem_inc(s["drained"], 2)
                if kind == "x":
                    for h, cols in halves():
                        act.wait_ge(s["filled"], 2 * p + h + 1)
                        if after(b, 0):
                            act.wait_ge(s["x_lo"], 2 * (b - 1) + h + 1)
                        act.activation(x32[:, cols], pg[:, h, :], ACT.Copy).then_inc(s["x_hi"], 1)
                        act.activation(xp[:, b % 2, h * TH:(h + 1) * TH, 0, :],
                                       pg[:, h, :].rearrange("p (t c) -> p t c", c=C), ACT.Copy).then_inc(s["x_hi"], 1)
                        act.wait_ge(s["x_hi"], 4 * b + 2 * h + 2)
                        act.sem_inc(s["drained"], 1)
                if kind == "key":
                    for h, cols in halves():
                        act.wait_ge(s["filled"], 2 * p + h + 1)
                        if h == 0 and after(b * TILES + t, KEYS - 1):
                            act.wait_ge(s["key_used"], b * TILES + t - KEYS + 1)
                        act.activation(key[:, t % KEYS, cols], pg[:, h, :], ACT.Copy).then_inc(s["drained"], 1)

            def count(b, t):
                k = b * TILES + t
                act.wait_ge(s["eyed"], k + 1)
                if after(k, 0):
                    act.wait_ge(s["counted"], k)
                act.activation(junk[:, :], H[:, t % HS, :], ACT.Copy, accum_out=dv[:, b, t:t + 1]).then_inc(s["counted"], 1)

            def copy_ht(b, t):
                k = b * TILES + t
                act.wait_ge(s["ht_psum"], k + 1)
                if t == 0 and after(b, 1):
                    act.wait_ge(s["o_ready"], 2 * (b - 1))
                act.activation(HT[:, b % 2, :, t * P:(t + 1) * P], pht[:, :, :], ACT.Copy).then_inc(s["ht_copied"], 1)

            def t_high(b):
                for h, cols in halves():
                    act.wait_ge(s["t_scaled"], 2 * b + h + 1)
                    if h == 0 and after(b, 0):
                        act.wait_ge(s["o_ready"], 2 * b)
                    act.activation(tp[:, 0, cols], t32[:, cols], ACT.Copy).then_inc(s["t_hi"], 1)

            def t_middle(b):
                for h, cols in halves():
                    act.wait_ge(s["t_res"], 2 * b + h + 1)
                    act.activation(tp[:, 1, cols], tr32[:, cols], ACT.Copy).then_inc(s["t_mid"], 1)

            def x_middle(b):
                for h in range(2):
                    act.wait_ge(s["x_res"], 2 * b + h + 1)
                    act.activation(xp[:, b % 2, h * TH:(h + 1) * TH, 1, :],
                                   xr32[:, h * HALF:(h + 1) * HALF].rearrange("p (t c) -> p t c", c=C),
                                   ACT.Copy).then_inc(s["x_mid"], 1)

            def copy_dv(b):
                for h in range(2):
                    act.wait_ge(s["dvb_psum"], 2 * b + h + 1)
                    act.activation(dvb[:, h * HALF:(h + 1) * HALF], po[:, h, :], ACT.Copy).then_inc(s["dvb_ready"], 1)

            group_sd(0, 0, 1)
            for f in first_pairs:
                drain(*f)
            x_middle(0)
            group_sd(1, 1, B)
            for t in range(LAG):
                count(0, t)

            def image(b, first, last):
                for t in range(TILES):
                    for f in pairs_of_step(b, t, last):
                        drain(*f)
                    if t + LAG < TILES:
                        count(b, t + LAG)
                    elif not last:
                        count(b + 1, t + LAG - TILES)
                    copy_ht(b, t)
                    if not first and t == 0:
                        copy_dv(b - 1)
                        t_high(b - 1)
                        t_middle(b - 1)
                    if t == 4 and not last:
                        x_middle(b + 1)
            images(image)
            copy_dv(B - 1)
            t_high(B - 1)
            t_middle(B - 1)
            act.wait_ge(s["stats_done"], 1)
            act.activation(bn_s[:, 0:1], bn_mv[:, 1:2], ACT.Sqrt, bias=eps_col[:, :]).then_inc(s["bn_sd"], 1)
            act.wait_ge(s["bn_affine"], 1)
            for b in range(B):
                act.activation(y[:, b, :], y[:, b, :], ACT.Silu, scale=bn_s[:, 2:3],
                               bias=bn_s[:, 3:4]).then_inc(s["silu_done"], 1)

        @block.gpsimd
        def _(pool):
            pool.memset(ones_b[:, :], 1.0).then_inc(s["setup"], 1)
            pool.memset(eps_col[:, :], GN_EPS).then_inc(s["setup"], 1)
            pool.wait_ge(s["const_in"], 16)
            pool.wait_ge(s["setup"], 2)
            pool.tensor_copy(ident_b[:, :], cst[:, C_IDENT:C_IDENT + P]).then_inc(s["setup"], 1)
            pool.wait_ge(s["w_in"], 16 * 5)
            pool.wait_ge(s["setup"], 3)
            pool.tensor_copy(bias_p1[:, 0, :], bias_row[:, :]).then_inc(s["bias_split"], 1)
            pool.wait_ge(s["bias_split"], 1)
            pool.tensor_tensor(bias_r[:, :], bias_row[:, :], bias_p1[:, 0, :], ALU.subtract).then_inc(s["setup"], 1)
            pool.wait_ge(s["setup"], 4)
            pool.tensor_copy(bias_p1[:, 1, :], bias_r[:, :]).then_inc(s["bias_split"], 1)
            pool.wait_ge(s["bias_split"], 2)
            pool.tensor_tensor(bias_p1[:, 2, :], bias_r[:, :], bias_p1[:, 1, :], ALU.subtract).then_inc(s["bias_split"], 1)

            def normalise(b):
                pool.tensor_scalar(xn[:, b, :], x_sb[:, b, :], gn_nm[:, b:b + 1], gn_rs[:, b:b + 1],
                                   ALU.add, ALU.mult).then_inc(s["xn_ready"], 1)

            def split_emb(b):
                pool.wait_ge(s["e_hi"], b + 1)
                if after(b, 0):
                    pool.wait_ge(s["lr_in"], LR_DMAS * b)
                pool.tensor_tensor(er32[:, :, :], e32[:, :, :], ep[:, 0, :, :], ALU.subtract).then_inc(s["e_res"], 1)
                pool.wait_ge(s["e_res"], b + 1)
                pool.tensor_copy(ep[:, 1, :, :], er32[:, :, :]).then_inc(s["e_mid"], 1)
                pool.wait_ge(s["e_mid"], b + 1)
                pool.tensor_tensor(ep[:, 2, :, :], er32[:, :, :], ep[:, 1, :, :], ALU.subtract).then_inc(s["e_lo"], 1)

            def x_tiles(a, h):
                return a[:, h * HALF:(h + 1) * HALF].rearrange("p (t c) -> p t c", c=C)

            def x_piece(b, h, q):
                return xp[:, b % 2, h * TH:(h + 1) * TH, q, :]

            def x_residual(b):
                for h in range(2):
                    pool.wait_ge(s["x_hi"], 4 * b + 2 * h + 2)
                    pool.tensor_tensor(x_tiles(xr32, h), x_tiles(x32, h), x_piece(b, h, 0), ALU.subtract)\
                        .then_inc(s["x_res"], 1)

            def x_low(b):
                for h in range(2):
                    pool.wait_ge(s["x_mid"], 2 * b + h + 1)
                    pool.tensor_tensor(x_piece(b, h, 2), x_tiles(xr32, h), x_piece(b, h, 1), ALU.subtract)\
                        .then_inc(s["x_lo"], 1)

            def split_t(b):
                for h, cols in halves():
                    pool.wait_ge(s["t_hi"], 2 * b + h + 1)
                    pool.tensor_tensor(tr32[:, cols], t32[:, cols], tp[:, 0, cols], ALU.subtract).then_inc(s["t_res"], 1)
                for h, cols in halves():
                    pool.wait_ge(s["t_mid"], 2 * b + h + 1)
                    pool.tensor_tensor(tp[:, 2, cols], tr32[:, cols], tp[:, 1, cols], ALU.subtract).then_inc(s["t_lo"], 1)

            def residual(b, h):
                pool.wait_ge(s["o_used"], 2 * b + h + 1)
                pool.tensor_tensor(y[:, b, h * HALF:(h + 1) * HALF], prod[:, h, :], xn[:, b, h * HALF:(h + 1) * HALF],
                                   ALU.add).then_inc(s["y_ready"], 1)

            def eye(b, t):
                k = b * TILES + t
                pool.wait_ge(s["masked"], k + 1)
                blk = H[:, t % HS, t * P:(t + 1) * P]
                pool.affine_select(out=blk, in_=blk, compare_op=ALU.not_equal, fill=1.0, base=0, pattern=[[-1, P]],
                                   channel_multiplier=1).then_inc(s["eyed"], 1)

            def flag(b, t):
                k = b * TILES + t
                pool.wait_ge(s["counted"], k + 1)
                if t == 0 and after(b, 0):
                    pool.wait_ge(s["checked"], k)
                pool.partition_all_reduce(most[:, t:t + 1], dv[:, b, t:t + 1], P, bass.bass_isa.ReduceOp.max)\
                    .then_inc(s["flagged"], 1)

            pool.wait_ge(s["gscale"], 1)
            pool.wait_ge(s["x_in0"], 16)
            normalise(0)
            split_emb(0)
            x_residual(0)
            x_low(0)
            pool.wait_ge(s["gscale"], 2)
            pool.wait_ge(s["x_in13"], 16)
            for b in range(1, B):
                normalise(b)
            for t in range(LAG):
                eye(0, t)
            flag(0, 0)

            def image(b, first, last):
                for t in range(TILES):
                    if t + LAG < TILES:
                        eye(b, t + LAG)
                    elif not last:
                        eye(b + 1, t + LAG - TILES)
                    if t + 1 < TILES:
                        flag(b, t + 1)
                    elif not last:
                        flag(b + 1, 0)
                    if not first and t == 0:
                        split_t(b - 1)
                    if not last and t == 1:
                        split_emb(b + 1)
                    if not last and t == 3:
                        x_residual(b + 1)
                    if not last and t == 4:
                        x_low(b + 1)
                    if not first and t in (4, 5):
                        residual(b - 1, t - 4)
            images(image)
            split_t(B - 1)
            for h in range(2):
                residual(B - 1, h)

        @block.vector
        def _(dve):
            chain = [0]

            def link(ins):
                chain[0] += 1
                ins.then_inc(s["step"], 1)
                dve.wait_ge(s["step"], chain[0])

            def group_stats(k, a, z):
                for b in range(a, z):
                    for h in range(2):
                        ins = dve.bn_stats(gn_stats[:, b, h, :], x_sb[:, b, h * HALF:(h + 1) * HALF])
                link(ins)
                for b in range(a, z):
                    ins = dve.bn_aggr(gn_mv[:, b, :], gn_stats[:, b, :, :])
                ins.then_inc(s["gstat"], 1)

            def group_scale(k, a, z):
                dve.wait_ge(s["gmean"], k + 1)
                dve.tensor_tensor(gn_dm[:, a:z], gn_mv[:, a:z, 0], po[:, 0, 0:z - a], ALU.subtract)
                link(dve.tensor_scalar(gn_nm[:, a:z], po[:, 0, 0:z - a], -1.0, None, ALU.mult))
                link(dve.tensor_tensor(gn_q[:, a:z], gn_dm[:, a:z], gn_dm[:, a:z], ALU.mult))
                dve.tensor_tensor(gn_q[:, a:z], gn_q[:, a:z], gn_mv[:, a:z, 1], ALU.add).then_inc(s["gdm"], 1)
                dve.wait_ge(s["gsd"], k + 1)
                dve.reciprocal(gn_rs[:, a:z], gn_sd[:, a:z]).then_inc(s["gscale"], 1)

            def mark(b, t, last):
                k = b * TILES + t
                dve.wait_ge(s["drained"], 2 * key_pair(b, t, last) + 2)
                for c in range(CHUNKS):
                    ins = dve.max(cand[:, c, :], key[:, t % KEYS, c * CHUNK:(c + 1) * CHUNK])
                link(ins)
                src = cand[:, :, :].rearrange("p c e -> p (c e)")
                for r in range(3):
                    link(dve.max(top[:, r, :], src))
                    if r < 2:
                        dst = cwork[:, r, :]
                        link(dve.match_replace(dst, top[:, r, :], src, 2 * FIRST_OUT))
                        src = dst
                link(dve.tensor_scalar(thr[:, :], top[:, 2, 7:8], 0.0, LAST_IN, ALU.min, ALU.max))
                if after(k, HS - 1):
                    dve.wait_ge(s["h_used"], k - HS + 1)
                dve.tensor_scalar(H[:, t % HS, :], key[:, t % KEYS, :], thr[:, :], None, ALU.is_ge).then_inc(s["masked"], 1)

            def release(b, t):
                k = b * TILES + t
                dve.wait_ge(s["flagged"], k + 1)
                over = dve.value_load(most[0:1, t:t + 1].bitcast(mybir.dt.int32))
                dve.sem_inc(s["checked"], 1)
                with dve.If(over > OVER_BITS):
                    pick(b, t)
                with dve.Else():
                    dve.nop()
                dve.sem_inc(s["h_ready"], 1)
                dve.sem_inc(s["key_used"], 1)

            def pick(b, t):
                steps = [0]

                def then(ins):
                    steps[0] += 1
                    ins.then_inc(s["slow_step"], 1)
                    dve.wait_ge(s["slow_step"], steps[0])

                then(dve.tensor_scalar(keyc[:, :], key[:, t % KEYS, :], 0.0, FIRST_OUT, ALU.min, ALU.max))
                src = keyc[:, :]
                for r in range(3):
                    then(dve.max(top[:, r, :], src))
                    then(dve.match_replace(work[:, :], top[:, r, :], src, FIRST_OUT))
                    src = work[:, :]
                then(dve.tensor_tensor(H[:, t % HS, :], keyc[:, :], work[:, :], ALU.is_gt))
                blk = H[:, t % HS, t * P:(t + 1) * P]
                then(dve.tensor_tensor(blk, blk, ident_b[:, :], ALU.max))
                then(dve.tensor_reduce(dv[:, b, t:t + 1], H[:, t % HS, :], AX.X, ALU.add))
                dve.sem_clear(s["slow_step"])

            def scale_t(b):
                dve.wait_ge(s["h_used"], TILES * (b + 1))
                if after(b, 0):
                    dve.wait_ge(s["t_lo"], 2 * b)
                link(dve.tensor_reduce(de[:, :], pd[:, 0:TILES * TILES].rearrange("p (t j) -> p j t", j=TILES),
                                       AX.X, ALU.add))
                link(dve.tensor_scalar(de[:, :], de[:, :], DEG_EPS, None, ALU.max))
                link(dve.reciprocal(rde[:, :], de[:, :]))
                for h in range(2):
                    js = slice(h * TH, (h + 1) * TH)
                    dve.tensor_tensor(t32[:, h * HALF:(h + 1) * HALF].rearrange("p (j c) -> p j c", c=C), pt[:, js, :],
                                      rde[:, js].unsqueeze(2).to_broadcast([P, TH, C]), ALU.mult).then_inc(s["t_scaled"], 1)

            def invert_dv(b):
                if after(b, 0):
                    dve.wait_ge(s["dvb_psum"], 2 * b)
                link(dve.tensor_scalar(rdv[:, :], dv[:, b, :], DEG_EPS, None, ALU.max))
                dve.reciprocal(rdv[:, :], rdv[:, :]).then_inc(s["rdv_ready"], 1)

            def out_half(b, h):
                dve.wait_ge(s["o_ready"], 2 * b + h + 1)
                if after(b, 0):
                    dve.wait_ge(s["y_ready"], 2 * (b - 1) + h + 1)
                dve.tensor_tensor(prod[:, h, :], po[:, h, :], dvb[:, h * HALF:(h + 1) * HALF],
                                  ALU.mult).then_inc(s["o_used"], 1)

            def y_stats(b, h):
                dve.wait_ge(s["y_ready"], 2 * b + h + 1)
                return dve.bn_stats(bn_st[:, 2 * b + h, :], y[:, b, h * HALF:(h + 1) * HALF])

            for q in range(2):
                dve.memset(lr[SQ_ROW:SQ_ROW + E, q, LB:RB + 1, :], 1.0).then_inc(s["ones_rows"], 1)
            dve.wait_ge(s["x_in0"], 16)
            group_stats(0, 0, 1)
            group_scale(0, 0, 1)
            dve.wait_ge(s["x_in13"], 16)
            group_stats(1, 1, B)
            group_scale(1, 1, B)

            def image(b, first, last):
                for t in range(TILES):
                    mark(b, t, last)
                    if t >= LAG:
                        release(b, t - LAG)
                    elif not first:
                        release(b - 1, t - LAG + TILES)
                        if t == LAG - 1:
                            invert_dv(b - 1)
                    if not first:
                        if t == 2:
                            scale_t(b - 1)
                        if t == 6:
                            out_half(b - 1, 0)
                        if t == 7:
                            out_half(b - 1, 1)
                            y_stats(b - 1, 0)
                            y_stats(b - 1, 1)
            images(image)
            for t in range(TILES - LAG, TILES):
                release(B - 1, t)
            invert_dv(B - 1)
            scale_t(B - 1)
            for h in range(2):
                out_half(B - 1, h)
            y_stats(B - 1, 0)
            link(y_stats(B - 1, 1))
            dve.bn_aggr(bn_mv[:, :], bn_st[:, :, :]).then_inc(s["stats_done"], 1)
            dve.wait_ge(s["bn_sd"], 1)
            dve.wait_ge(s["w_in"], 16 * 5)
            link(dve.reciprocal(bn_s[:, 1:2], bn_s[:, 0:1]))
            link(dve.tensor_tensor(bn_s[:, 2:3], bn_s[:, 1:2], gb[:, 0:1], ALU.mult))
            link(dve.tensor_tensor(bn_s[:, 0:1], bn_s[:, 2:3], bn_mv[:, 0:1], ALU.mult))
            dve.tensor_tensor(bn_s[:, 3:4], gb[:, 1:2], bn_s[:, 0:1], ALU.subtract).then_inc(s["bn_affine"], 1)
            for b in range(B):
                dve.wait_ge(s["silu_done"], b + 1)
                dve.tensor_tensor(y[:, b, :], y[:, b, :], x_sb[:, b, :], ALU.add).then_inc(s["sum_done"], 1)


def kernel(x, L0_conv_fc_w, L0_conv_fc_b, L0_conv_dist_w, L0_conv_bn_gamma, L0_conv_bn_beta):
    import concourse.bacc as bacc
    from concourse.bass_utils import run_bass_kernel_spmd

    arrays = {
        "x": np.ascontiguousarray(x).reshape(B, C, N),
        "fc_wT": np.ascontiguousarray(np.transpose(L0_conv_fc_w)),
        "fc_b": np.ascontiguousarray(L0_conv_fc_b).reshape(1, C),
        "dist_wT": np.ascontiguousarray(np.transpose(L0_conv_dist_w)),
        "gamma": np.ascontiguousarray(L0_conv_bn_gamma).reshape(C, 1),
        "beta": np.ascontiguousarray(L0_conv_bn_beta).reshape(C, 1),
        "const": constants(),
    }
    nc = bacc.Bacc("TRN2", target_bir_lowering=False, num_devices=1)
    args = [nc.dram_tensor(k, a.shape, mybir.dt.from_np(a.dtype), kind="ExternalInput").ap()
            for k, a in arrays.items()]
    out = nc.dram_tensor("out", (B, C, N), F32, kind="ExternalOutput").ap()
    scratch = nc.dram_tensor("scratch", (P, PIECES, 2, QN), BF16, kind="Internal").ap()
    build(nc, *args, scratch, out)
    r = run_bass_kernel_spmd(nc, [arrays], core_ids=[0])
    return r.results[0]["out"].reshape(B, C, 32, 32)
```

```python
from contextlib import ExitStack

import concourse.bass as bass
from concourse import mybir
from concourse.alu_op_type import AluOpType as ALU
import numpy as np

ACT = mybir.ActivationFunctionType
AX = mybir.AxisListType
F32 = mybir.dt.float32
BF16 = mybir.dt.bfloat16

P = 128
B, C, N, E = 4, 128, 1024, 32
TILES = N // P
HALF = N // 2
TH = TILES // 2
PIECES = 3
NEAREST = 24
CHUNK = 64
CHUNKS = N // CHUNK
GROUP = 4
GN_EPS, BN_EPS, DEG_EPS = 1e-5, 1e-5, 1e-9
assert GN_EPS == BN_EPS
KEYS = 8
HS = 8
LAG = 2
AHEAD = 6
T_BLOCKS = HALF // (C + 1)
T_BANKS = -(-TILES // T_BLOCKS)
X_STEP, EMB_STEP = 1, 4
POOL_SUMS = (1, 2)
WEIGHT_DMAS = 5
Q = P // E
QN = N // Q

LAST_IN = -float(np.nextafter(np.float32(100), np.float32(200))) / 2
FIRST_OUT = -float(np.nextafter(np.float32(-2 * LAST_IN), np.float32(200))) / 2
OVER_BITS = int(np.float32(NEAREST + 0.5).view(np.int32))

C_GROUP, C_IDENT, C_SQ, C_HI, C_MID = 0, P, 2 * P, 3 * P, 3 * P + 1
C_END = C_MID + 1
LA, RA, LB, RB = range(4)
SQ_ROW = 2 * E
K_B = SQ_ROW + 2 * PIECES


def constants():
    c = np.zeros((P, C_END), np.float32)
    c[:, C_GROUP:C_GROUP + P] = np.kron(np.eye(P // GROUP), np.full((GROUP, GROUP), 1.0 / GROUP))
    c[:, C_IDENT:C_IDENT + P] = np.eye(P)
    c[:, C_SQ:C_SQ + P] = np.kron(np.eye(Q), np.full((E, E), -0.5))
    for i in range(2 * PIECES):
        c[SQ_ROW + i, C_HI] = -1.0 if i % PIECES > 0 else 0.0
        c[SQ_ROW + i, C_MID] = -1.0 if i % PIECES > 1 else 0.0
    return c


def halves():
    return [(h, slice(h * HALF, (h + 1) * HALF)) for h in range(2)]


def build(nc, x, fc_wT, fc_b, dist_wT, gamma, beta, const, scratch, out):
    ctx = ExitStack()
    with ctx:
        def sb(name, shape, dt=F32):
            return ctx.enter_context(nc.sbuf_tensor(name, shape, dt))

        def ps(name, shape, dt=F32):
            return ctx.enter_context(nc.psum_tensor(name, shape, dt))

        def sem(name):
            return ctx.enter_context(nc.semaphore(name))

        x_sb = sb("x_sb", [P, B, N])
        xn = sb("xn", [P, B, N])
        y = xn
        cst = sb("cst", [P, C_END])
        wT = sb("wT", [P, C])
        dT = sb("dT", [P, E])
        dT4 = sb("dT4", [P, Q, E])
        gb = sb("gb", [P, 2])
        bias = sb("bias", [P, 1])
        ident_b = sb("ident_b", [P, P], BF16)
        gn_stats = sb("gn_stats", [P, B, 2, 6])
        gn_mv = sb("gn_mv", [P, B, 2])
        gn_dm = sb("gn_dm", [P, B])
        gn_q = sb("gn_q", [P, B])
        gn_nm = sb("gn_nm", [P, B])
        gn_sd = sb("gn_sd", [P, B])
        gn_rs = sb("gn_rs", [P, B])
        eps_col = sb("eps_col", [P, 1])
        esq = sb("esq", [P, QN])
        e32 = sb("e32", [P, 2, QN])
        er32 = sb("er32", [P, 2, QN])
        ep = sb("ep", [P, PIECES, 2, QN], BF16)
        lr = sb("lr", [P, 2, 4, N], BF16)
        x32 = sb("x32", [P, N])
        xr32 = sb("xr32", [P, N])
        xp = sb("xp", [P, 2, TILES, PIECES * C + 1], BF16)
        key = sb("key", [P, KEYS, N])
        cand = sb("cand", [P, 2, CHUNKS, 8])
        cwork = sb("cwork", [P, 2, CHUNKS * 8])
        top = sb("top", [P, 3, 8])
        thr = sb("thr", [P, 1])
        work = sb("work", [P, N])
        H = sb("H", [P, HS, N], BF16)
        junk = sb("junk", [P, N], BF16)
        most = sb("most", [P, TILES])
        HT = sb("HT", [P, 2, TILES, N], BF16)
        dv = sb("dv", [P, B, TILES])
        rdv = sb("rdv", [P, TILES])
        rde = sb("rde", [P, TILES])
        t32 = sb("t32", [P, N])
        tr32 = sb("tr32", [P, N])
        tp = sb("tp", [P, 2, PIECES, N], BF16)
        dvb = sb("dvb", [P, N])
        dvb_last = x32
        prod = sb("prod", [P, 2, HALF])
        bn_st = sb("bn_st", [P, B * 2, 6])
        bn_mv = sb("bn_mv", [P, 2])
        warm = sb("warm", [P, 1])
        centre = sb("centre", [P, 2])
        bn_s = sb("bn_s", [P, 4])
        esq0, er0, nr0 = dvb[0:E, :], t32[0:2 * E, :], tr32[SQ_ROW:SQ_ROW + E, :]
        n0_piece = junk[SQ_ROW:SQ_ROW + E, :]

        pg = ps("pg", [P, 2, HALF])
        pt = ps("pt", [P, T_BANKS, HALF])
        pht = ps("pht", [P, TILES, P], BF16)
        po = ps("po", [P, 2, HALF])

        names = ("const_in w_in x_in0 x_in1 x_in23 e1_filled n1_filled out_done setup ones_rows gstat gmean gdm "
                 "gvar gsd gscale xn_ready filled drained e_sq e_copied e_hi e_res e_mid e_lo ep_out lr_in x_hi "
                 "x_res x_mid x_lo masked eyed counted flagged checked key_used h_ready ht_psum ht_copied h_used "
                 "t_scaled t_hi t_res t_mid t_lo t_lo_last t_res_last rdv_ready dvb_psum dvb_ready o_ready "
                 "o_used y_ready step slow_step stats_done bn_sd bn_affine silu_done sum_dve sum_pool xn0_ready "
                 "dT_spread e0_sq e0_hi e0_res e0_mid e0_lo e0_left e0_right e0_again left0_made n0_filled n0_hi "
                 "n0_res n0_mid n0_right n0_ones").split()
        s = {n: sem("s_" + n) for n in names}

        def x_cols(b, t, q, wide=C):
            at = q * C + (q > 0)
            return xp[:, b % 2, t, at:at + wide]

        T_GROUPS = [[(0, 3), (3, 1)], [(4, 2), (6, 2)]]
        LR_DMAS = 16 * 14

        block = ctx.enter_context(nc.Block())

        first_pairs = [("emb0", 0, 0), ("key", 0, 0), ("key", 0, 1), ("key", 0, 2), ("x", 0, 0)] + \
                      [("key", 0, t) for t in range(3, AHEAD)]

        def pairs_of_step(b, t):
            got = []
            k = b * TILES + t + AHEAD
            if k < B * TILES:
                got.append(("key", k // TILES, k % TILES))
            if t == X_STEP and b + 1 < B:
                got.append(("x", b + 1, 0))
            if t == EMB_STEP and b + 2 < B:
                got.append(("emb", b + 2, 0))
            return got

        pair = {f: p for p, f in enumerate(first_pairs + [f for b in range(B) for t in range(TILES)
                                                           for f in pairs_of_step(b, t)])}

        def silus_before(b, h):
            return [1, 2, 3, 3, 4, 4, 5, 6][2 * b + h]

        def images(body):
            for b in range(B):
                body(b, b == 0, b == B - 1)

        @block.sync
        def _(sp):
            sp.dma_start(x_sb[:, 0, :], x[0]).then_inc(s["x_in0"], 16)
            sp.dma_start(cst[:, :], const).then_inc(s["const_in"], 16)
            sp.wait_ge(s["x_in0"], 16)
            sp.dma_start(x_sb[:, 1, :], x[1]).then_inc(s["x_in1"], 16)
            sp.dma_start(x_sb[:, 2:B, :], x[2:B].rearrange("b c n -> c b n")).then_inc(s["x_in23"], 16)

            def place(b):
                q = b % 2
                if b > 1:
                    sp.wait_ge(s["filled"], 2 * pair["key", b - 2, TILES - 1] + 2)
                sp.wait_ge(s["e_lo"], b)
                if b > 1:
                    sp.wait_ge(s["lr_in"], LR_DMAS * (b - 1))
                sp.dma_start(scratch, ep[:, :, :, :]).then_inc(s["ep_out"], 16)
                sp.wait_ge(s["ep_out"], 16 * b)
                emb = scratch[:, :, 0, :].rearrange("(q e) p c -> p e q c", e=E)
                nsq = scratch[0:P:E, :, 1, :].rearrange("q p c -> p q c")
                for k, row, piece in ((LA, 0, 0), (LA, 1, 0), (LA, 2, 0), (LA, 3, 1), (RA, 3, 0), (LB, 0, 1), (LB, 1, 2),
                                      (RB, 0, 1), (RB, 1, 0)):
                    sp.dma_start(lr[row * E:(row + 1) * E, q, k, :], emb[piece]).then_inc(s["lr_in"], 16)
                for piece in range(PIECES):
                    sp.dma_start(lr[piece * E:(piece + 1) * E, q, RA, :], emb[piece]).then_inc(s["lr_in"], 16)
                sp.dma_start(lr[SQ_ROW:SQ_ROW + PIECES, q, LB, :], nsq).then_inc(s["lr_in"], 16)
                sp.dma_start(lr[SQ_ROW + PIECES:K_B, q, RB, :], nsq).then_inc(s["lr_in"], 16)

            sp.wait_ge(s["ones_rows"], 3)

            def image(b, first, last):
                if not last:
                    place(b + 1)
            images(image)
            sums = {"sum_dve": 0, "sum_pool": 0}
            for b in range(B):
                for h, cols in halves():
                    by = "sum_pool" if h == 1 and b in POOL_SUMS else "sum_dve"
                    sums[by] += 1
                    sp.wait_ge(s[by], sums[by])
                    sp.dma_start(out[b, :, cols], y[:, b, cols]).then_inc(s["out_done"], 16)
            sp.wait_ge(s["out_done"], 16 * 2 * B)

        @block.tensor
        def _(pe):
            ident = cst[:, C_IDENT:C_IDENT + P]
            group = cst[:, C_GROUP:C_GROUP + P]
            sqsum = cst[:, C_SQ:C_SQ + P]

            def group_means(k, a, z):
                pe.wait_ge(s["gstat"], k + 1)
                pe.matmul(pt[:, T_BANKS - 1, 0:z - a], group, gn_mv[:, a:z, 0], start=True, stop=True).then_inc(s["gmean"], 1)

            def group_variances(k, a, z):
                pe.wait_ge(s["gdm"], k + 1)
                pe.matmul(pt[:, T_BANKS - 1, B:B + z - a], group, gn_q[:, a:z], start=True, stop=True).then_inc(s["gvar"], 1)

            def embed(b, into):
                pe.wait_ge(s["xn_ready"], b)
                for q in range(Q):
                    mm = pe.matmul(into[q * E:(q + 1) * E, :], dT[:, :], xn[:, b, q * QN:(q + 1) * QN],
                                   start=True, stop=True)
                return mm

            def norms(b, into):
                pe.wait_ge(s["e_sq"], b)
                return pe.matmul(into, sqsum, esq[:, :], start=True, stop=True)

            def fill(kind, b, t):
                p = pair[kind, b, t]

                def bank_free(h):
                    if p > 0:
                        pe.wait_ge(s["drained"], 2 * (p - 1) + h + 1)
                if kind == "emb0":
                    pe.wait_ge(s["dT_spread"], 1)
                    pe.wait_ge(s["xn0_ready"], 1)
                    for h, cols in halves():
                        pe.matmul(pg[:, h, :], dT4[:, :, :].rearrange("p q e -> p (q e)"), xn[:, 0, cols],
                                  start=True, stop=True).then_inc(s["filled"], 1)
                        if h == 0:
                            group_means(1, 1, 2)
                    for h, cols in halves():
                        pe.wait_ge(s["e0_sq"], h + 1)
                        pe.matmul(pt[SQ_ROW:SQ_ROW + E, h, :], cst[0:E, C_SQ:C_SQ + E], esq0[:, cols],
                                  start=True, stop=True).then_inc(s["n0_filled"], 1)
                if kind == "emb":
                    bank_free(0)
                    embed(b, pg[:, 0, 0:QN]).then_inc(s["filled"], 1)
                if kind == "x":
                    for h, cols in halves():
                        bank_free(h)
                        for i in range(TH):
                            o = pg[:, h, i * C:(i + 1) * C]
                            n = h * HALF + i * P
                            mm = pe.matmul(o, xn[:, b, n:n + P], wT[:, :], start=True, stop=True, skip_group_check=True)
                        mm.then_inc(s["filled"], 1)
                if kind == "key":
                    if t == 0 and b > 0:
                        pe.wait_ge(s["lr_in"], LR_DMAS * b)
                    for h, cols in halves():
                        if t == TH and h == 0 and b <= 0:
                            pe.wait_ge(s["left0_made"], 2)
                        if t == 0 and b <= 0:
                            pe.wait_ge(s["e0_right"], h + 1)
                            pe.wait_ge(s["e0_lo"], h + 1)
                            pe.wait_ge(s["e0_again"], h + 1)
                            pe.wait_ge(s["n0_ones"], h + 1)
                            pe.wait_ge(s["left0_made"], 1)
                        bank_free(h)
                        for k, rows, start in ((LA, P, True), (LB, K_B, False)):
                            mm = pe.matmul(pg[:, h, :], lr[0:rows, b % 2, k, t * P:(t + 1) * P],
                                           lr[0:rows, b % 2, k + 1, cols], start=start, stop=not start)
                        mm.then_inc(s["filled"], 1)

            def fill_norms(b):
                pe.wait_ge(s["drained"], 2 * pair["emb", b, 0])
                norms(b, pg[:, 1, 0:QN]).then_inc(s["filled"], 1)

            def transpose(b, t):
                k = b * TILES + t
                pe.wait_ge(s["h_ready"], k + 1)
                if k > 0:
                    pe.wait_ge(s["ht_copied"], k)
                for j in range(TILES):
                    mm = pe.transpose(pht[:, j, :], H[:, t % HS, j * P:(j + 1) * P], ident_b[:, :])
                mm.then_inc(s["ht_psum"], 1)

            def scatter(b, t):
                if t == 0:
                    pe.wait_ge(s["x_lo"], 2 * (b + 1))
                    if b > 0:
                        pe.wait_ge(s["t_scaled"], 2 * b)
                for j in range(TILES):
                    lhs = H[:, t % HS, j * P:(j + 1) * P]
                    at = j % T_BLOCKS * (C + 1)
                    for q in range(PIECES):
                        wide = C + 1 if q == 0 else C
                        mm = pe.matmul(pt[:, j // T_BLOCKS, at:at + wide], lhs, x_cols(b, t, q, wide),
                                       start=(t == 0 and j % T_BLOCKS == 0 and q == 0),
                                       stop=(t == TILES - 1 and q == PIECES - 1), skip_group_check=True)
                mm.then_inc(s["h_used"], 1)

            def spread_dv(b):
                pe.wait_ge(s["rdv_ready"], b + 1)
                for h in range(2):
                    if b == B - 1:
                        pe.wait_ge(s["drained"], 2 * len(pair) - 1 + h)
                    elif b > 0:
                        pe.wait_ge(s["o_used"], 2 * (b - 1) + h + 1)
                    for i in range(TH):
                        t = h * TH + i
                        mm = pe.matmul((pg if b == B - 1 else po)[:, h, i * P:(i + 1) * P],
                                       rdv[:, t:t + 1].to_broadcast([P, P]), ident,
                                       start=True, stop=True, skip_group_check=True)
                    mm.then_inc(s["dvb_psum"], 1)

            def gather(b, h):
                if b == B - 1:
                    pe.wait_ge(s["o_used"], 2 * (b - 1) + h + 1)
                    if h == 0:
                        pe.wait_ge(s["t_lo_last"], 2)
                else:
                    pe.wait_ge(s["dvb_ready"], 2 * b + h + 1)
                    if h == 0:
                        pe.wait_ge(s["t_lo"], 2 * (b + 1))
                if h == 0:
                    pe.wait_ge(s["ht_copied"], TILES * (b + 1))
                for j in range(TILES):
                    for q in range(PIECES):
                        mm = pe.matmul(po[:, h, :], tp[:, b % 2, q, j * C:(j + 1) * C],
                                       HT[:, b % 2, j, h * HALF:(h + 1) * HALF],
                                       start=(j == 0 and q == 0), stop=(j == TILES - 1 and q == PIECES - 1))
                mm.then_inc(s["o_ready"], 1)

            pe.wait_ge(s["const_in"], 16)
            group_means(0, 0, 1)
            group_variances(0, 0, 1)
            pe.wait_ge(s["w_in"], 16 * WEIGHT_DMAS)
            for f in first_pairs:
                if f[0] == "x":
                    pe.wait_ge(s["setup"], 2)
                    pe.wait_ge(s["ones_rows"], 3)
                fill(*f)
                if f[0] == "emb0":
                    group_variances(1, 1, 2)
                    embed(1, po[:, 0, 0:QN]).then_inc(s["e1_filled"], 1)
                    norms(1, po[:, 1, 0:QN]).then_inc(s["n1_filled"], 1)
                if f[0] == "key" and f[2] == 2:
                    group_means(2, 2, B)
                if f[0] == "key" and f[2] == AHEAD - 1:
                    group_variances(2, 2, B)

            def image(b, first, last):
                for t in range(TILES):
                    pairs = pairs_of_step(b, t)
                    for f in pairs[:1]:
                        fill(*f)
                    transpose(b, t)
                    if not first and t == 0:
                        spread_dv(b - 1)
                    if last and t == TILES - 1:
                        spread_dv(b)
                    for f in pairs[1:]:
                        fill(*f)
                    scatter(b, t)
                    if t == EMB_STEP and b + 2 < B:
                        fill_norms(b + 2)
                    if not first and t == (2 if last else 3):
                        gather(b - 1, 0)
                    if not first and t == (TILES - 1 if last else 4):
                        gather(b - 1, 1)
            images(image)
            for h in range(2):
                gather(B - 1, h)

        @block.scalar
        def _(act):
            act.dma_start(dT[:, :], dist_wT).then_inc(s["w_in"], 16)
            act.dma_start(wT[:, :], fc_wT).then_inc(s["w_in"], 16)
            act.dma_start(bias[:, :], fc_b).then_inc(s["w_in"], 16)
            act.dma_start(gb[:, 0:1], gamma).then_inc(s["w_in"], 16)
            act.dma_start(gb[:, 1:2], beta).then_inc(s["w_in"], 16)
            act.wait_ge(s["setup"], 1)
            act.activation(warm[:, :], eps_col[:, :], ACT.Sqrt)

            def group_sd(k, a, z):
                act.wait_ge(s["gvar"], k + 1)
                act.activation(gn_sd[:, a:z], pt[:, T_BANKS - 1, B:B + z - a], ACT.Sqrt, bias=eps_col[:, :]).then_inc(s["gsd"], 1)

            def drain(kind, b, t):
                p = pair[kind, b, t]
                if kind == "emb0":
                    for h, cols in halves():
                        act.wait_ge(s["filled"], 2 * p + h + 1)
                        act.activation(esq0[:, cols], pg[0:E, h, :], ACT.Square).then_inc(s["e0_sq"], 1)
                        act.activation(lr[:, 0, LA, cols], pg[:, h, :], ACT.Copy).then_inc(s["e0_hi"], 1)
                    group_sd(1, 1, 2)
                    for h, cols in halves():
                        act.wait_ge(s["n0_filled"], h + 1)
                        act.activation(n0_piece[:, cols], pt[SQ_ROW:SQ_ROW + E, h, :], ACT.Copy).then_inc(s["n0_hi"], 1)
                        act.wait_ge(s["e0_res"], h + 1)
                        act.activation(lr[0:2 * E, 0, RA, cols], er0[:, cols], ACT.Copy).then_inc(s["e0_mid"], 1)
                        act.activation(lr[2 * E:P, 0, RA, cols], pg[2 * E:P, h, :], ACT.Copy)
                        act.activation(lr[E:2 * E, 0, RB, cols], pg[E:2 * E, h, :], ACT.Copy).then_inc(s["e0_again"], 1)
                        act.wait_ge(s["n0_res"], h + 1)
                        act.activation(n0_piece[:, cols], nr0[:, cols], ACT.Copy).then_inc(s["n0_mid"], 1)
                    act.wait_ge(s["e1_filled"], 1)
                    act.activation(esq[:, :], po[:, 0, 0:QN], ACT.Square).then_inc(s["e_sq"], 1)
                    act.wait_ge(s["n1_filled"], 1)
                    high_emb(1, po)
                    for h in range(2):
                        act.wait_ge(s["e0_again"], h + 1)
                        act.wait_ge(s["e0_left"], h + 1)
                        act.sem_inc(s["drained"], 1)
                if kind == "emb":
                    act.wait_ge(s["filled"], 2 * p + 1)
                    act.activation(esq[:, :], pg[:, 0, 0:QN], ACT.Square).then_inc(s["e_sq"], 1)
                if kind == "x":
                    for h, cols in halves():
                        act.wait_ge(s["filled"], 2 * p + h + 1)
                        if b > 0:
                            act.wait_ge(s["x_lo"], 2 * (b - 1) + h + 1)
                        act.activation(x32[:, cols], pg[:, h, :], ACT.Copy).then_inc(s["x_hi"], 1)
                        act.wait_ge(s["x_hi"], 4 * b + 2 * h + 1)
                        act.sem_inc(s["drained"], 1)
                        act.activation(x_cols(b, slice(h * TH, (h + 1) * TH), 0),
                                       x32[:, cols].rearrange("p (t c) -> p t c", c=C), ACT.Copy).then_inc(s["x_hi"], 1)
                if kind == "key":
                    for h, cols in halves():
                        act.wait_ge(s["filled"], 2 * p + h + 1)
                        if h == 0 and b * TILES + t >= KEYS:
                            act.wait_ge(s["key_used"], b * TILES + t - KEYS + 1)
                        act.activation(key[:, t % KEYS, cols], pg[:, h, :], ACT.Copy).then_inc(s["drained"], 1)

            def high_emb(b, banks):
                act.activation(e32[:, :, :], banks[:, :, 0:QN], ACT.Copy).then_inc(s["e_copied"], 1)
                act.wait_ge(s["e_copied"], b)
                if b > 1:
                    act.sem_inc(s["drained"], 2)
                act.activation(ep[:, 0, :, :], e32[:, :, :], ACT.Copy).then_inc(s["e_hi"], 1)

            def drain_norms(b):
                act.wait_ge(s["filled"], 2 * pair["emb", b, 0] + 2)
                if b > 1:
                    act.wait_ge(s["e_lo"], b - 1)
                    act.wait_ge(s["ep_out"], 16 * (b - 1))
                high_emb(b, pg)

            def middle_emb(b):
                act.wait_ge(s["e_res"], b)
                act.activation(ep[:, 1, :, :], er32[:, :, :], ACT.Copy).then_inc(s["e_mid"], 1)

            def count(b, t):
                k = b * TILES + t
                act.wait_ge(s["eyed"], k + 1)
                if k > 0:
                    act.wait_ge(s["counted"], k)
                act.activation(junk[:, :], H[:, t % HS, :], ACT.Copy, accum_out=dv[:, b, t:t + 1]).then_inc(s["counted"], 1)

            def count_ahead(b, t, last):
                if t + LAG < TILES:
                    count(b, t + LAG)
                elif not last:
                    count(b + 1, t + LAG - TILES)

            def copy_ht(b, t):
                k = b * TILES + t
                act.wait_ge(s["ht_psum"], k + 1)
                if t == 0 and b > 1:
                    act.wait_ge(s["o_ready"], 2 * (b - 1))
                act.activation(HT[:, b % 2, :, t * P:(t + 1) * P], pht[:, :, :], ACT.Copy).then_inc(s["ht_copied"], 1)

            def t_high(b):
                for h, cols in halves():
                    act.wait_ge(s["t_scaled"], 2 * b + h + 1)
                    if h == 0 and b > 1:
                        act.wait_ge(s["o_ready"], 2 * (b - 1))
                    act.activation(tp[:, b % 2, 0, cols], t32[:, cols], ACT.Copy).then_inc(s["t_hi"], 1)

            def t_middle(b):
                for h, cols in halves():
                    if b == B - 1:
                        act.wait_ge(s["t_res_last"], h + 1)
                    else:
                        act.wait_ge(s["t_res"], 2 * b + h + 1)
                    act.activation(tp[:, b % 2, 1, cols], tr32[:, cols], ACT.Copy).then_inc(s["t_mid"], 1)

            def x_middle(b):
                for h in range(2):
                    act.wait_ge(s["x_res"], 2 * b + h + 1)
                    act.activation(x_cols(b, slice(h * TH, (h + 1) * TH), 1),
                                   xr32[:, h * HALF:(h + 1) * HALF].rearrange("p (t c) -> p t c", c=C),
                                   ACT.Copy).then_inc(s["x_mid"], 1)

            def copy_dv(b):
                for h in range(2):
                    act.wait_ge(s["dvb_psum"], 2 * b + h + 1)
                    if b == B - 1:
                        act.wait_ge(s["x_lo"], 2 * B)
                    into, banks = (dvb_last, pg) if b == B - 1 else (dvb, po)
                    act.activation(into[:, h * HALF:(h + 1) * HALF], banks[:, h, :], ACT.Copy).then_inc(s["dvb_ready"], 1)

            group_sd(0, 0, 1)
            for f in first_pairs:
                drain(*f)
                if f[0] == "key" and f[2] == 0:
                    middle_emb(1)
                if f[0] == "key" and f[2] == 3:
                    x_middle(0)
                if f[0] == "key" and f[2] >= AHEAD - LAG:
                    count(0, f[2] - AHEAD + LAG)
            group_sd(2, 2, B)

            def image(b, first, last):
                for t in range(TILES):
                    pairs = pairs_of_step(b, t)
                    if t != X_STEP:
                        count_ahead(b, t, last)
                    for f in pairs[:1]:
                        drain(*f)
                    if t == X_STEP:
                        count_ahead(b, t, last)
                    for f in pairs[1:]:
                        drain(*f)
                    copy_ht(b, t)
                    if not first and t == 0:
                        copy_dv(b - 1)
                    if last and t == TILES - 1:
                        copy_dv(b)
                    if t == EMB_STEP and b + 2 < B:
                        drain_norms(b + 2)
                    if not first and t == 0:
                        t_high(b - 1)
                    if not first and t == 1:
                        t_middle(b - 1)
                    if t == X_STEP + 1 and not last:
                        x_middle(b + 1)
                    if t == EMB_STEP + 1 and b + 2 < B:
                        middle_emb(b + 2)
            images(image)
            t_high(B - 1)
            t_middle(B - 1)
            act.wait_ge(s["stats_done"], 1)
            act.activation(bn_s[:, 0:1], bn_mv[:, 1:2], ACT.Sqrt, bias=eps_col[:, :]).then_inc(s["bn_sd"], 1)
            act.wait_ge(s["bn_affine"], 1)
            for b in range(B):
                for h, cols in halves() if b in (0, B - 1) else [(0, slice(0, N))]:
                    act.activation(y[:, b, cols], y[:, b, cols], ACT.Silu, scale=bn_s[:, 2:3],
                                   bias=bn_s[:, 3:4]).then_inc(s["silu_done"], 1)

        @block.gpsimd
        def _(pool):
            pool.memset(eps_col[:, :], GN_EPS).then_inc(s["setup"], 1)
            pool.wait_ge(s["const_in"], 16)
            pool.wait_ge(s["setup"], 1)
            pool.tensor_copy(ident_b[:, :], cst[:, C_IDENT:C_IDENT + P]).then_inc(s["setup"], 1)
            pool.wait_ge(s["w_in"], 16 * WEIGHT_DMAS)
            pool.tensor_copy(dT4[:, :, :], dT[:, :].unsqueeze(1).to_broadcast([P, Q, E])).then_inc(s["dT_spread"], 1)

            def normalise(b):
                pool.tensor_scalar(xn[:, b, :], x_sb[:, b, :], gn_nm[:, b:b + 1], gn_rs[:, b:b + 1],
                                   ALU.add, ALU.mult).then_inc(s["xn_ready"], 1)

            def split_emb(b):
                pool.wait_ge(s["e_hi"], b)
                pool.tensor_tensor(er32[:, :, :], e32[:, :, :], ep[:, 0, :, :], ALU.subtract).then_inc(s["e_res"], 1)

            def low_emb(b):
                pool.wait_ge(s["e_mid"], b)
                pool.tensor_tensor(ep[:, 2, :, :], er32[:, :, :], ep[:, 1, :, :], ALU.subtract).then_inc(s["e_lo"], 1)

            def x_tiles(a, h):
                return a[:, h * HALF:(h + 1) * HALF].rearrange("p (t c) -> p t c", c=C)

            def x_piece(b, h, q):
                return x_cols(b, slice(h * TH, (h + 1) * TH), q)

            def x_residual(b):
                for h in range(2):
                    pool.wait_ge(s["x_hi"], 4 * b + 2 * h + 2)
                    pool.tensor_tensor(x_tiles(xr32, h), x_tiles(x32, h), x_piece(b, h, 0), ALU.subtract)\
                        .then_inc(s["x_res"], 1)

            def x_low(b):
                for h in range(2):
                    pool.wait_ge(s["x_mid"], 2 * b + h + 1)
                    pool.tensor_tensor(x_piece(b, h, 2), x_tiles(xr32, h), x_piece(b, h, 1), ALU.subtract)\
                        .then_inc(s["x_lo"], 1)

            def t_residual(b):
                for h, cols in halves():
                    pool.wait_ge(s["t_hi"], 2 * b + h + 1)
                    pool.tensor_tensor(tr32[:, cols], t32[:, cols], tp[:, b % 2, 0, cols], ALU.subtract)\
                        .then_inc(s["t_res"], 1)

            def t_low(b):
                for h, cols in halves():
                    pool.wait_ge(s["t_mid"], 2 * b + h + 1)
                    pool.tensor_tensor(tp[:, b % 2, 2, cols], tr32[:, cols], tp[:, b % 2, 1, cols], ALU.subtract)\
                        .then_inc(s["t_lo"], 1)

            def residual(b, h):
                pool.wait_ge(s["o_used"], 2 * b + h + 1)
                pool.tensor_tensor(y[:, b, h * HALF:(h + 1) * HALF], prod[:, h, :], xn[:, b, h * HALF:(h + 1) * HALF],
                                   ALU.add).then_inc(s["y_ready"], 1)

            def eye(b, t):
                k = b * TILES + t
                pool.wait_ge(s["masked"], k + 1)
                blk = H[:, t % HS, t * P:(t + 1) * P]
                pool.affine_select(out=blk, in_=blk, compare_op=ALU.not_equal, fill=1.0, base=0, pattern=[[-1, P]],
                                   channel_multiplier=1).then_inc(s["eyed"], 1)

            def flag(b, t):
                k = b * TILES + t
                pool.wait_ge(s["counted"], k + 1)
                if t == 0 and b > 0:
                    pool.wait_ge(s["checked"], k)
                pool.partition_all_reduce(most[:, t:t + 1], dv[:, b, t:t + 1], P, bass.bass_isa.ReduceOp.max)\
                    .then_inc(s["flagged"], 1)

            pool.wait_ge(s["gscale"], 2)
            pool.wait_ge(s["x_in1"], 16)
            normalise(1)
            pool.wait_ge(s["xn_ready"], 1)
            for h, cols in halves():
                pool.wait_ge(s["n0_right"], h + 1)
                pool.memset(lr[SQ_ROW:SQ_ROW + PIECES, 0, RB, cols], 1.0).then_inc(s["n0_ones"], 1)
            pool.wait_ge(s["n0_ones"], 2)
            split_emb(1)
            low_emb(1)
            x_residual(0)
            eye(0, 0)
            x_low(0)
            eye(0, 1)
            flag(0, 0)

            def image(b, first, last):
                for t in range(TILES):
                    if t + LAG < TILES:
                        eye(b, t + LAG)
                    elif not last:
                        eye(b + 1, t + LAG - TILES)
                    if t + 1 < TILES:
                        flag(b, t + 1)
                    elif not last:
                        flag(b + 1, 0)
                    if first and t in (1, 2):
                        if t == 1:
                            pool.wait_ge(s["gscale"], 3)
                            pool.wait_ge(s["x_in23"], 16)
                        normalise(t + 1)
                    if not first and t == 1:
                        t_residual(b - 1)
                    if not first and t == 2:
                        t_low(b - 1)
                    if t == EMB_STEP + 1 and b + 2 < B:
                        split_emb(b + 2)
                    if t == EMB_STEP + 2 and b + 2 < B:
                        low_emb(b + 2)
                    if not last and t == X_STEP + 1:
                        x_residual(b + 1)
                    if not last and t == X_STEP + 2:
                        x_low(b + 1)
                    if b > 1 and t == 0:
                        residual(b - 2, 0)
                    if b > 1 and t == 0:
                        residual(b - 2, 1)
            images(image)
            for h in range(2):
                residual(B - 2, h)
            for b in POOL_SUMS:
                pool.wait_ge(s["silu_done"], silus_before(b, 1))
                pool.tensor_tensor(y[:, b, HALF:N], y[:, b, HALF:N], x_sb[:, b, HALF:N], ALU.add).then_inc(s["sum_pool"], 1)

        @block.vector
        def _(dve):
            chain = [0]

            def signal(ins):
                chain[0] += 1
                ins.then_inc(s["step"], 1)
                return chain[0]

            def link(ins):
                dve.wait_ge(s["step"], signal(ins))

            def group_stats(k, a, z):
                for b in range(a, z):
                    for h in range(2):
                        ins = dve.bn_stats(gn_stats[:, b, h, :], x_sb[:, b, h * HALF:(h + 1) * HALF])
                link(ins)
                for b in range(a, z):
                    ins = dve.bn_aggr(gn_mv[:, b, :], gn_stats[:, b, :, :])
                ins.then_inc(s["gstat"], 1)

            def group_scale(k, a, z):
                dve.wait_ge(s["gmean"], k + 1)
                dve.tensor_tensor(gn_dm[:, a:z], gn_mv[:, a:z, 0], pt[:, T_BANKS - 1, 0:z - a], ALU.subtract)
                link(dve.tensor_scalar(gn_nm[:, a:z], pt[:, T_BANKS - 1, 0:z - a], -1.0, None, ALU.mult))
                link(dve.tensor_tensor(gn_q[:, a:z], gn_dm[:, a:z], gn_dm[:, a:z], ALU.mult))
                dve.tensor_tensor(gn_q[:, a:z], gn_q[:, a:z], gn_mv[:, a:z, 1], ALU.add).then_inc(s["gdm"], 1)

            def group_inverse(k, a, z):
                dve.wait_ge(s["gsd"], k + 1)
                dve.reciprocal(gn_rs[:, a:z], gn_sd[:, a:z]).then_inc(s["gscale"], 1)

            def candidates(b, t, chunks):
                if 0 in chunks:
                    dve.wait_ge(s["drained"], 2 * pair["key", b, t] + 2)
                for c in chunks:
                    ins = dve.max(cand[:, t % 2, c, :], key[:, t % KEYS, c * CHUNK:(c + 1) * CHUNK])
                if CHUNKS - 1 in chunks:
                    signal(ins)

            def mark(b, t, last):
                k = b * TILES + t

                def ahead(first, end):
                    if t + 1 < TILES:
                        candidates(b, t + 1, range(first, end))
                    elif not last:
                        candidates(b + 1, 0, range(first, end))

                src = cand[:, t % 2, :, :].rearrange("p c e -> p (c e)")
                dve.wait_ge(s["step"], chain[0])
                for r in range(3):
                    found = signal(dve.max(top[:, r, :], src))
                    ahead(4 * r, 4 * r + 2)
                    dve.wait_ge(s["step"], found)
                    if r < 2:
                        dst = cwork[:, r, :]
                        replaced = signal(dve.match_replace(dst, top[:, r, :], src, 2 * FIRST_OUT))
                        ahead(4 * r + 2, 4 * r + 4)
                        dve.wait_ge(s["step"], replaced)
                        src = dst
                limited = signal(dve.tensor_scalar(thr[:, :], top[:, 2, 7:8], 0.0, LAST_IN, ALU.min, ALU.max))
                ahead(10, CHUNKS)
                dve.wait_ge(s["step"], limited)
                if k >= HS:
                    dve.wait_ge(s["h_used"], k - HS + 1)
                dve.tensor_scalar(H[:, t % HS, :], key[:, t % KEYS, :], thr[:, :], None, ALU.is_ge).then_inc(s["masked"], 1)

            def release(b, t):
                k = b * TILES + t
                dve.wait_ge(s["flagged"], k + 1)
                over = dve.value_load(most[0:1, t:t + 1].bitcast(mybir.dt.int32))
                dve.sem_inc(s["checked"], 1)
                with dve.If(over > OVER_BITS):
                    pick(b, t)
                with dve.Else():
                    dve.nop()
                dve.sem_inc(s["h_ready"], 1)
                dve.sem_inc(s["key_used"], 1)

            def pick(b, t):
                keyc = key[:, t % KEYS, :]
                steps = [0]

                def then(ins):
                    steps[0] += 1
                    ins.then_inc(s["slow_step"], 1)
                    dve.wait_ge(s["slow_step"], steps[0])

                then(dve.tensor_scalar(keyc, keyc, 0.0, FIRST_OUT, ALU.min, ALU.max))
                src = keyc
                for r in range(3):
                    then(dve.max(top[:, r, :], src))
                    then(dve.match_replace(work[:, :], top[:, r, :], src, FIRST_OUT))
                    src = work[:, :]
                then(dve.tensor_tensor(H[:, t % HS, :], keyc, work[:, :], ALU.is_gt))
                blk = H[:, t % HS, t * P:(t + 1) * P]
                then(dve.tensor_tensor(blk, blk, ident_b[:, :], ALU.max))
                then(dve.tensor_reduce(dv[:, b, t:t + 1], H[:, t % HS, :], AX.X, ALU.add))
                dve.sem_clear(s["slow_step"])

            def scale_t(b):
                dve.wait_ge(s["h_used"], TILES * (b + 1))
                if b > 0:
                    dve.wait_ge(s["t_lo"], 2 * b)
                full = TILES // T_BLOCKS
                for js, banks, n in ((slice(0, full * T_BLOCKS), slice(0, full), T_BLOCKS),
                                     (slice(full * T_BLOCKS, TILES), slice(full, T_BANKS), TILES - full * T_BLOCKS)):
                    cols = pt[:, banks, C:n * (C + 1):C + 1]
                    ins = dve.tensor_scalar(rde[:, js].rearrange("p (a n) -> p a n", n=n), cols, DEG_EPS, None, ALU.max)
                link(ins)
                link(dve.reciprocal(rde[:, :], rde[:, :]))
                for h, groups in enumerate(T_GROUPS):
                    for j, n in groups:
                        blocks = pt[:, j // T_BLOCKS, j % T_BLOCKS * (C + 1):(j % T_BLOCKS + n) * (C + 1)]
                        ins = dve.tensor_tensor(t32[:, j * C:(j + n) * C].rearrange("p (j c) -> p j c", c=C),
                                                blocks.rearrange("p (j c) -> p j c", c=C + 1)[:, :, 0:C],
                                                rde[:, j:j + n].unsqueeze(2).to_broadcast([P, n, C]), ALU.mult)
                    ins.then_inc(s["t_scaled"], 1)

            def split_last_t(b):
                for h, cols in halves():
                    dve.wait_ge(s["t_hi"], 2 * b + h + 1)
                    dve.tensor_tensor(tr32[:, cols], t32[:, cols], tp[:, b % 2, 0, cols], ALU.subtract)\
                        .then_inc(s["t_res_last"], 1)
                for h, cols in halves():
                    dve.wait_ge(s["t_mid"], 2 * b + h + 1)
                    dve.tensor_tensor(tp[:, b % 2, 2, cols], tr32[:, cols], tp[:, b % 2, 1, cols], ALU.subtract)\
                        .then_inc(s["t_lo_last"], 1)

            def invert_dv(b):
                if b > 0:
                    dve.wait_ge(s["dvb_psum"], 2 * b)
                link(dve.tensor_scalar(rdv[:, :], dv[:, b, :], DEG_EPS, None, ALU.max))
                dve.reciprocal(rdv[:, :], rdv[:, :]).then_inc(s["rdv_ready"], 1)

            def out_half(b, h):
                dve.wait_ge(s["o_ready"], 2 * b + h + 1)
                if b > 0:
                    dve.wait_ge(s["y_ready"], 2 * (b - 1) + h + 1)
                if b == B - 1:
                    dve.wait_ge(s["dvb_ready"], 2 * b + h + 1)
                by = dvb_last if b == B - 1 else dvb
                dve.tensor_tensor(prod[:, h, :], po[:, h, :], by[:, h * HALF:(h + 1) * HALF],
                                  ALU.mult).then_inc(s["o_used"], 1)

            def y_stats(b, h):
                dve.wait_ge(s["y_ready"], 2 * b + h + 1)
                return dve.bn_stats(bn_st[:, 2 * b + h, :], y[:, b, h * HALF:(h + 1) * HALF])

            for q in range(2):
                dve.memset(lr[SQ_ROW:SQ_ROW + E, q, LB:RB + 1, :], 1.0).then_inc(s["ones_rows"], 1)
            dve.memset(xp[:, :, :, C:C + 1], 1.0).then_inc(s["ones_rows"], 1)
            dve.wait_ge(s["x_in0"], 16)
            group_stats(0, 0, 1)
            group_scale(0, 0, 1)
            group_inverse(0, 0, 1)
            dve.wait_ge(s["gscale"], 1)
            dve.tensor_scalar(xn[:, 0, :], x_sb[:, 0, :], gn_nm[:, 0:1], gn_rs[:, 0:1], ALU.add, ALU.mult)\
                .then_inc(s["xn0_ready"], 1)
            dve.wait_ge(s["x_in1"], 16)
            group_stats(1, 1, 2)
            group_scale(1, 1, 2)

            def norm_rows(k, rows, cols):
                part = slice(SQ_ROW, SQ_ROW + rows)
                return dve.scalar_tensor_tensor(lr[part, 0, k, cols], junk[part, cols], cst[part, C_MID:C_MID + 1],
                                                tr32[part, cols], ALU.mult, ALU.add)

            def left0(h, cols):
                dve.tensor_tensor(lr[3 * E:P, 0, LA, cols], pg[3 * E:P, h, :], lr[3 * E:P, 0, LA, cols], ALU.subtract)\
                    .then_inc(s["e0_left"], 1)
                dve.wait_ge(s["n0_mid"], h + 1)
                dve.wait_ge(s["e0_lo"], h + 1)
                norm_rows(LB, PIECES, cols)
                dve.tensor_copy(lr[0:2 * E, 0, LB, cols], lr[0:2 * E, 0, RA, cols]).then_inc(s["left0_made"], 1)

            for h, cols in halves():
                dve.wait_ge(s["e0_hi"], h + 1)
                dve.tensor_tensor(er0[:, cols], pg[0:2 * E, h, :], lr[0:2 * E, 0, LA, cols], ALU.subtract)\
                    .then_inc(s["e0_res"], 1)
            group_inverse(1, 1, 2)
            for h, cols in halves():
                dve.wait_ge(s["n0_hi"], h + 1)
                dve.scalar_tensor_tensor(nr0[:, cols], n0_piece[:, cols], cst[SQ_ROW:SQ_ROW + E, C_HI:C_HI + 1],
                                         pt[SQ_ROW:SQ_ROW + E, h, :], ALU.mult, ALU.add).then_inc(s["n0_res"], 1)
                dve.wait_ge(s["e0_mid"], h + 1)
                dve.tensor_copy(lr[0:E, 0, RB, cols], lr[0:E, 0, RA, cols]).then_inc(s["e0_right"], 1)
                dve.tensor_tensor(lr[E:2 * E, 0, RA, cols], er0[E:2 * E, cols], lr[E:2 * E, 0, RA, cols], ALU.subtract)\
                    .then_inc(s["e0_lo"], 1)
            for h, cols in halves():
                dve.wait_ge(s["n0_mid"], h + 1)
                dve.wait_ge(s["n0_res"], h + 1)
                norm_rows(RB, 2 * PIECES, cols).then_inc(s["n0_right"], 1)
                if h == 0:
                    left0(h, cols)
            left0(*halves()[1])
            dve.wait_ge(s["x_in23"], 16)
            group_stats(2, 2, B)
            candidates(0, 0, range(CHUNKS))

            def image(b, first, last):
                for t in range(TILES):
                    mark(b, t, last)
                    if first and t == 1:
                        group_scale(2, 2, B)
                    if first and t == 2:
                        group_inverse(2, 2, B)
                    if t >= LAG:
                        release(b, t - LAG)
                    elif not first:
                        release(b - 1, t - LAG + TILES)
                        if t == LAG - 1:
                            invert_dv(b - 1)
                    if not first:
                        if t == 2:
                            scale_t(b - 1)
                            if b > 1:
                                out_half(b - 2, 1)
                    if b > 1 and t == 0:
                        out_half(b - 2, 0)
                    if b > 1 and not last and t == 4:
                        y_stats(b - 2, 0)
                        y_stats(b - 2, 1)
            images(image)
            for h in range(2):
                y_stats(B - 3, h)
            for t in range(TILES - LAG, TILES):
                release(B - 1, t)
            invert_dv(B - 1)
            out_half(B - 2, 0)
            scale_t(B - 1)
            split_last_t(B - 1)
            out_half(B - 2, 1)
            for h in range(2):
                y_stats(B - 2, h)
            for h, cols in halves():
                out_half(B - 1, h)
                dve.wait_ge(s["o_used"], 2 * B - 1 + h)
                link(dve.tensor_tensor(y[:, B - 1, cols], prod[:, h, :], xn[:, B - 1, cols], ALU.add))
                ins = dve.bn_stats(bn_st[:, 2 * (B - 1) + h, :], y[:, B - 1, cols])
            link(ins)
            dve.bn_aggr(bn_mv[:, :], bn_st[:, :, :]).then_inc(s["stats_done"], 1)
            dve.wait_ge(s["w_in"], 16 * WEIGHT_DMAS)
            dve.wait_ge(s["stats_done"], 1)
            link(dve.tensor_tensor(centre[:, 0:1], bn_mv[:, 0:1], bias[:, :], ALU.add))
            dve.tensor_tensor(centre[:, 1:2], bias[:, :], centre[:, 0:1], ALU.subtract)
            dve.wait_ge(s["bn_sd"], 1)
            link(dve.reciprocal(bn_s[:, 1:2], bn_s[:, 0:1]))
            link(dve.tensor_tensor(bn_s[:, 2:3], bn_s[:, 1:2], gb[:, 0:1], ALU.mult))
            link(dve.tensor_tensor(bn_s[:, 0:1], bn_s[:, 2:3], centre[:, 1:2], ALU.mult))
            dve.tensor_tensor(bn_s[:, 3:4], gb[:, 1:2], bn_s[:, 0:1], ALU.add).then_inc(s["bn_affine"], 1)
            for b in range(B):
                for h, cols in halves():
                    if h == 0 or b not in POOL_SUMS:
                        dve.wait_ge(s["silu_done"], silus_before(b, h))
                        dve.tensor_tensor(y[:, b, cols], y[:, b, cols], x_sb[:, b, cols], ALU.add)\
                            .then_inc(s["sum_dve"], 1)


def kernel(x, L0_conv_fc_w, L0_conv_fc_b, L0_conv_dist_w, L0_conv_bn_gamma, L0_conv_bn_beta):
    import concourse.bacc as bacc
    from concourse.bass_utils import run_bass_kernel_spmd

    arrays = {
        "x": np.ascontiguousarray(x).reshape(B, C, N),
        "fc_wT": np.ascontiguousarray(np.transpose(L0_conv_fc_w)),
        "fc_b": np.ascontiguousarray(L0_conv_fc_b).reshape(C, 1),
        "dist_wT": np.ascontiguousarray(np.transpose(L0_conv_dist_w)),
        "gamma": np.ascontiguousarray(L0_conv_bn_gamma).reshape(C, 1),
        "beta": np.ascontiguousarray(L0_conv_bn_beta).reshape(C, 1),
        "const": constants(),
    }
    nc = bacc.Bacc("TRN2", target_bir_lowering=False, num_devices=1)
    args = [nc.dram_tensor(k, a.shape, mybir.dt.from_np(a.dtype), kind="ExternalInput").ap()
            for k, a in arrays.items()]
    out = nc.dram_tensor("out", (B, C, N), F32, kind="ExternalOutput").ap()
    scratch = nc.dram_tensor("scratch", (P, PIECES, 2, QN), BF16, kind="Internal").ap()
    build(nc, *args, scratch, out)
    r = run_bass_kernel_spmd(nc, [arrays], core_ids=[0])
    return r.results[0]["out"].reshape(B, C, 32, 32)
```
